# Optimizing a Trainium2 kernel written in Bass

```python
import numpy as np
import jax
import jax.numpy as jnp

def _softmax(x, axis=-1):
    return jax.nn.softmax(x, axis=axis)

def _gelu(x):
    return jax.nn.gelu(x, approximate=True)

def _silu(x):
    return jax.nn.silu(x)

def _sigmoid(x):
    return jax.nn.sigmoid(x)

def _layernorm(x, axis=-1, eps=1e-05):
    m = jnp.mean(x, axis=axis, keepdims=True)
    v = jnp.var(x, axis=axis, keepdims=True)
    return (x - m) / jnp.sqrt(v + eps)

def _scatter_add(tgt, idx, src, axis=0):
    return tgt.at[idx].add(src)

def _segment_sum(src, seg, n):
    return jax.ops.segment_sum(src, seg, n)
kernel_name = 'mk_decoder_preln_d1_seqx_r2_9893c3'

def setup_inputs(seed: int=0):
    np.random.seed(seed)
    _w = jnp.asarray

    def _rec_inputs():
        import jax
        import jax.numpy as jnp
        _rk = jax.random.key(seed)
        x = 7.22e-05 + 1 * jax.random.normal(jax.random.fold_in(_rk, 1), (8, 512, 512), jnp.float32)
        _lenS = 512 - jax.random.randint(jax.random.fold_in(_rk, 7), (8,), 0, max(1, 512 // 4) + 1, jnp.int32)
        _lenS2 = 512 - jax.random.randint(jax.random.fold_in(_rk, 8), (8,), 0, max(1, 512 // 4) + 1, jnp.int32)
        _ctx_1024P = jax.random.normal(jax.random.fold_in(_rk, 11), (8, 16, 512), jnp.float32)
        _ctx_1024c = jax.random.dirichlet(jax.random.fold_in(_rk, 511), 0.3 * jnp.ones((16,), jnp.float32), (8, 512))
        _ctx_1024t = jnp.einsum('bsk,bkd->bsd', _ctx_1024c, _ctx_1024P)
        _ctx_1024t = _ctx_1024t * jax.lax.rsqrt(jnp.mean(jnp.square(_ctx_1024t)) + 1e-12) * 0.953939
        ctx_1024 = 4.13588e-05 + 0.999923 * (_ctx_1024t + 0.3 * jax.random.normal(jax.random.fold_in(_rk, 611), (8, 512, 512), jnp.float32))
        return (x, ctx_1024)
    x, ctx_1024 = _rec_inputs()

    def _L0_attn_setup():
        import jax, jax.numpy as jnp
        import numpy as np
        key = jax.random.key(seed)
        k1, k2, k3 = jax.random.split(key, 3)
        bs, seqlen, hidden = (2, 1024, 512)
        s, h = (4, 128)
        std = 0.02
        num_layers = 12
        hidden_states = jax.random.normal(k1, (bs, seqlen, hidden), dtype=jnp.float32)
        q_scale = 1.0 / np.sqrt(2.0 * num_layers * h)
        queries = jax.random.normal(k2, (s, h, h * s), dtype=jnp.float32) * std * q_scale
        combiners = jax.random.normal(k3, (s, h * s, h), dtype=jnp.float32) * (std * q_scale)
        return {'hidden_states': hidden_states, 'queries': queries, 'combiners': combiners}
    _L0_attn_all = _L0_attn_setup()
    _L0_attn_in = {k: v for k, v in _L0_attn_all.items() if k in ('queries', 'combiners')}
    del _L0_attn_all

    def _L0_xattn_setup():
        import jax, jax.numpy as jnp
        import numpy as np
        B, S, E, A = (4, 1024, 512, 512)
        key = jax.random.key(seed)
        ks = jax.random.split(key, 6)
        scale = 1.0 / np.sqrt(E)
        return {'query': jax.random.normal(ks[0], (B, S, E), jnp.float32), 'key': jax.random.normal(ks[1], (B, S, E), jnp.float32), 'value': jax.random.normal(ks[2], (B, S, E), jnp.float32), 'Wq': jax.random.normal(ks[3], (E, A), jnp.float32) * scale, 'bq': jnp.zeros((A,), jnp.float32), 'Wk': jax.random.normal(ks[4], (E, A), jnp.float32) * scale, 'bk': jnp.zeros((A,), jnp.float32), 'Wv': jax.random.normal(ks[5], (E, A), jnp.float32) * scale, 'bv': jnp.zeros((A,), jnp.float32)}
    _L0_xattn_all = _L0_xattn_setup()
    _L0_xattn_in = {k: v for k, v in _L0_xattn_all.items() if k in ('Wq', 'bq', 'Wk', 'bk', 'Wv', 'bv')}
    del _L0_xattn_all

    def _L0_ffn_setup():
        import jax, jax.numpy as jnp
        import numpy as np
        B, S, D = (1, 1024, 512)
        F = 704
        E = 16
        K = 2
        CAP_FACTOR = 1.25

        def _mlp(h, wg, wu, wd):
            return jax.nn.silu(h @ wg) * (h @ wu) @ wd
        key = jax.random.key(seed)
        ks = jax.random.split(key, 10)
        sd = 0.02
        return {'x': jax.random.normal(ks[0], (B, S, D), jnp.float32), 'router_w': jax.random.normal(ks[1], (D, E), jnp.float32) * sd, 'router_b': jnp.zeros((E,), jnp.float32), 'w_gate': jax.random.normal(ks[2], (E, D, F), jnp.float32) * sd, 'w_up': jax.random.normal(ks[3], (E, D, F), jnp.float32) * sd, 'w_down': jax.random.normal(ks[4], (E, F, D), jnp.float32) * sd, 'sw_gate': jax.random.normal(ks[5], (D, F), jnp.float32) * sd, 'sw_up': jax.random.normal(ks[6], (D, F), jnp.float32) * sd, 'sw_down': jax.random.normal(ks[7], (F, D), jnp.float32) * sd}
    _L0_ffn_all = _L0_ffn_setup()
    _L0_ffn_in = {k: v for k, v in _L0_ffn_all.items() if k in ('router_w', 'router_b', 'w_gate', 'w_up', 'w_down', 'sw_gate', 'sw_up', 'sw_down')}
    del _L0_ffn_all
    return {'x': x, 'ctx_1024': ctx_1024, 'L0_attn_queries': _L0_attn_in['queries'], 'L0_attn_combiners': _L0_attn_in['combiners'], 'L0_xattn_Wq': _L0_xattn_in['Wq'], 'L0_xattn_bq': _L0_xattn_in['bq'], 'L0_xattn_Wk': _L0_xattn_in['Wk'], 'L0_xattn_bk': _L0_xattn_in['bk'], 'L0_xattn_Wv': _L0_xattn_in['Wv'], 'L0_xattn_bv': _L0_xattn_in['bv'], 'L0_ffn_router_w': _L0_ffn_in['router_w'], 'L0_ffn_router_b': _L0_ffn_in['router_b'], 'L0_ffn_w_gate': _L0_ffn_in['w_gate'], 'L0_ffn_w_up': _L0_ffn_in['w_up'], 'L0_ffn_w_down': _L0_ffn_in['w_down'], 'L0_ffn_sw_gate': _L0_ffn_in['sw_gate'], 'L0_ffn_sw_up': _L0_ffn_in['sw_up'], 'L0_ffn_sw_down': _L0_ffn_in['sw_down']}

def reference(x, ctx_1024, L0_attn_queries, L0_attn_combiners, L0_xattn_Wq, L0_xattn_bq, L0_xattn_Wk, L0_xattn_bk, L0_xattn_Wv, L0_xattn_bv, L0_ffn_router_w, L0_ffn_router_b, L0_ffn_w_gate, L0_ffn_w_up, L0_ffn_w_down, L0_ffn_sw_gate, L0_ffn_sw_up, L0_ffn_sw_down):
    import jax
    import jax.numpy as jnp

    def _L0_attn_ref(hidden_states, queries, combiners):
        import jax, jax.numpy as jnp
        import numpy as np
        s, h, _ = queries.shape
        bs, S, E = hidden_states.shape
        x = hidden_states.reshape(bs, S, s, h)
        qw = queries.reshape(s, h, s, h)
        Q = jnp.einsum('btae,aeqf->qbtaf', x, qw)
        pre = jnp.einsum('qbtaf,buqf->qbtau', Q, x)
        attn = jnp.einsum('qbtau,buqg->abtqg', pre, x)
        attn = attn.reshape(s, bs, S, s * h)
        out = jnp.einsum('abtk,akg->btag', attn, combiners)
        return out.reshape(bs, S, s * h)

    def _L0_xattn_ref(query, key, value, Wq, bq, Wk, bk, Wv, bv):
        import jax, jax.numpy as jnp
        import numpy as np
        B, S, E, A = (4, 1024, 512, 512)
        q = jnp.einsum('bse,ea->bsa', query, Wq) + bq
        k = jnp.einsum('bse,ea->bsa', key, Wk) + bk
        v = jnp.einsum('bse,ea->bsa', value, Wv) + bv
        inv_sqrt_d = 1.0 / jnp.sqrt(jnp.asarray(A, q.dtype))
        scores = jnp.einsum('bqa,bka->bqk', q, k) * inv_sqrt_d
        probs = jax.nn.softmax(scores, axis=-1)
        return jnp.einsum('bqk,bka->bqa', probs, v)

    def _L0_ffn_ref(x, router_w, router_b, w_gate, w_up, w_down, sw_gate, sw_up, sw_down):
        import jax, jax.numpy as jnp
        import numpy as np
        B, S, D = (1, 1024, 512)
        F = 704
        E = 16
        K = 2
        CAP_FACTOR = 1.25

        def _mlp(h, wg, wu, wd):
            return jax.nn.silu(h @ wg) * (h @ wu) @ wd
        b, s, d = x.shape
        N = b * s
        NK = N * K
        C = int(np.ceil(CAP_FACTOR * NK / E))
        x_tokens = x.reshape(N, d)
        logits = x_tokens @ router_w + router_b
        probs = jax.nn.softmax(logits, axis=-1)
        vals, idx = jax.lax.top_k(probs, K)
        vals = vals / (jnp.sum(vals, axis=-1, keepdims=True) + 1e-09)
        idx_flat = idx.reshape(NK)
        vals_flat = vals.reshape(NK)
        oh_e = jax.nn.one_hot(idx_flat, E, dtype=x.dtype)
        pos = (jnp.cumsum(oh_e, axis=0) * oh_e).sum(axis=1) - 1
        within = (pos < C).astype(x.dtype)
        pos_c = jnp.clip(pos, 0, C - 1).astype(jnp.int32)
        token_ids = jnp.arange(NK) // K
        x_pair = x_tokens[token_ids] * within[:, None]
        expert_inputs = jnp.zeros((E, C, d), x.dtype).at[idx_flat, pos_c].add(x_pair)
        expert_outputs = jax.vmap(_mlp)(expert_inputs, w_gate, w_up, w_down)
        gathered = expert_outputs[idx_flat, pos_c] * (vals_flat * within)[:, None]
        output_tokens = gathered.reshape(N, K, d).sum(axis=1)
        return x + _mlp(x, sw_gate, sw_up, sw_down) + output_tokens.reshape(b, s, d)
    x = x + _L0_attn_ref(_layernorm(x, axis=-1), L0_attn_queries, L0_attn_combiners)
    x = x + _L0_xattn_ref(_layernorm(x, axis=-1), ctx_1024, ctx_1024, L0_xattn_Wq, L0_xattn_bq, L0_xattn_Wk, L0_xattn_bk, L0_xattn_Wv, L0_xattn_bv)
    x = x + _L0_ffn_ref(_layernorm(x, axis=-1), L0_ffn_router_w, L0_ffn_router_b, L0_ffn_w_gate, L0_ffn_w_up, L0_ffn_w_down, L0_ffn_sw_gate, L0_ffn_sw_up, L0_ffn_sw_down)
    return x

_drawn_inputs = setup_inputs


def setup_inputs(seed=0):
    import zlib

    import numpy as np

    out = dict(_drawn_inputs(seed))
    spreads = {'L0_xattn_bq': (0.0, 0.41),
     'L0_xattn_bk': (0.0, 0.8),
     'L0_xattn_bv': (0.0, 0.1),
     'L0_ffn_router_b': (0.0, 0.774)}
    factors = {'L0_attn_queries': 3.213,
     'L0_attn_combiners': 3.169,
     'L0_ffn_router_w': 3.258,
     'L0_ffn_w_gate': 3.095,
     'L0_ffn_w_up': 3.024,
     'L0_ffn_w_down': 3.032}
    for name, (base, spread) in spreads.items():
        noise = np.random.default_rng([zlib.crc32(name.encode()), seed]).standard_normal(out[name].shape)
        drawn = base * np.exp(spread * noise) if base else spread * noise
        out[name] = jnp.asarray(drawn.astype(out[name].dtype))
    for name, factor in factors.items():
        out[name] = (out[name] * factor).astype(out[name].dtype)
    return out
```

```python
from contextlib import ExitStack

import concourse.bass as bass
from concourse import mybir

F32 = mybir.dt.float32
F32R = mybir.dt.float32r
BF16 = mybir.dt.bfloat16
I32 = mybir.dt.int32
U32 = mybir.dt.uint32
ALU = mybir.AluOpType
ACT = mybir.ActivationFunctionType
AX_X = mybir.AxisListType.X

P = 128
B, S, D = 8, 512, 512
NT = S // P
NC = D // P
H = NC
N = B * S
E, K, F = 16, 2, 704
CAP = -(-5 * N * K // (4 * E))
ET = CAP // P
NSLOT = E * ET
FC = -(-F // P)
FH = F - (FC - 1) * P
GU = 2 * (FC - 1) + 1
WC = GU + FC
PAD = CAP
EPS = 1e-5
SCALE = float(D) ** -0.5
BANKS = 8


def three_pass(pe, out, parts):
    last = None
    todo = []
    for lh, ll, rh, rl in parts:
        todo += [(lh, rh), (lh, rl), (ll, rh)]
    for i, (left, right) in enumerate(todo):
        last = pe.matmul(out, left, right, start=(i == 0), stop=(i == len(todo) - 1))
    return last


def build(nc, a):
    Y = nc.dram_tensor("tokens_normed", (N + PAD, D), F32, kind="Internal").ap()
    with ExitStack() as keep:
        def sb(name, shape, dt):
            return keep.enter_context(nc.sbuf_tensor(name, shape, dt))

        shared = {
            "ident": sb("ident", [P, P], F32),
            "slot_list": sb("slot_list", [P, 2 * NSLOT], F32),
            "slot_index": sb("slot_index", [P, NSLOT], U32),
        }
        phase1(nc, a, Y, shared)
        phase2(nc, a, Y, shared)


def phase1(nc, a, Y, shared):
    out = a["out"]
    ident, slot_list, slot_index = shared["ident"], shared["slot_list"], shared["slot_index"]
    with ExitStack() as ctx:
        def sb(name, shape, dt):
            return ctx.enter_context(nc.sbuf_tensor(name, shape, dt))

        def sem(name):
            return ctx.enter_context(nc.semaphore(name))

        ps = [ctx.enter_context(nc.psum_tensor(f"ps_a{i}", [P, 512], F32)) for i in range(BANKS)]
        BANK = {"V": (0, 1, 2, 3), "Y1T": (4, 5, 6, 7), "Y2T": (0, 1, 2, 3), "L": (4,), "Q": (5, 6, 7, 0),
                "X": (1,), "G": (2,), "YT": (3, 4, 5, 6), "SC": (7, 0, 1, 2), "Z": (3,), "T": (4, 5, 6, 7),
                "PT": (0, 1, 2, 3), "M": (4,), "PV": (5, 6, 7, 0), "A": (1, 2, 3, 4),
                "W": (0, 1, 2, 3), "KR": (4,), "QB": (5,)}
        s_mm = {k: ctx.enter_context(nc.semaphore(f"s_mm_{k}")) for k in BANK}
        s_ev = {k: ctx.enter_context(nc.semaphore(f"s_ev_{k}")) for k in BANK}

        def filled(eng, step, b, i=0):
            eng.wait_ge(s_mm[step], len(BANK[step]) * b + i + 1)

        def drained(eng, step, b, i=0):
            if 0 <= b < B:
                eng.wait_ge(s_ev[step], len(BANK[step]) * b + i + 1)

        WH, WL = sb("WH", [P, NC, D], F32R), sb("WL", [P, NC, D], F32R)
        VWH, VWL = sb("VWH", [P, NC, D], F32R), sb("VWL", [P, NC, D], F32R)
        QT = sb("QT", [P, H, H, P], F32)
        CT = sb("CT", [P, H, H * P], F32)
        bv_all = sb("bv_all", [P, D], F32)
        key_row = sb("key_row", [P, D], F32)
        rw = sb("rw", [P, NC, E], F32)
        rb_all = sb("rb_all", [P, E], F32)
        bias_col = sb("bias_col", [P, 2 * NC], F32)
        qbias = sb("qbias", [P, 2 * NC + 1], F32)
        before = sb("before", [P, P], BF16)
        ones = sb("ones", [P, P], BF16)
        iota_lo = sb("iota_lo", [P, P], F32)
        iota_e = sb("iota_e", [P, E], F32)
        token_no = sb("token_no", [P, B * NT], F32)
        pad_no = sb("pad_no", [P, NSLOT], F32)
        magic = sb("magic", [P, NT], I32)
        x = [sb(f"x{i}", [P, NT, D], F32) for i in range(2)]
        y = sb("y", [P, NT, D], F32)
        yT = sb("yT", [P, NC, S], F32)
        G = sb("G", [P, H * P], F32)
        M = sb("M", [P, H * P], F32)
        y1h, y1l = sb("y1h", [P, NC, S], F32R), sb("y1l", [P, NC, S], F32R)
        qh, ql = sb("qh", [P, NC, S], F32R), sb("ql", [P, NC, S], F32R)
        craw = sb("craw", [P, NC, S], F32)
        ch, cl = sb("ch", [P, NC, S], F32R), sb("cl", [P, NC, S], F32R)
        vh, vl = sb("vh", [P, NT, D], F32R), sb("vl", [P, NT, D], F32R)
        vtmp = [sb(f"vtmp{i}", [P, D], F32) for i in range(2)]
        prob = sb("prob", [P, NT, S], F32)
        ph, pl = sb("ph", [P, NT, S], F32R), sb("pl", [P, NT, S], F32R)
        y2 = sb("y2", [P, NT, D], F32)
        junk = y2
        stats = sb("stats", [P, NT, 6], F32)
        mv = sb("mv", [P, NT, 2], F32)
        veps, rstd, rt = (sb(n, [P, NT], F32) for n in ("veps", "rstd", "rt"))
        krow, smax, mr, nbias, rsum, rinv = (sb(n, [P, NT], F32) for n in ("krow", "smax", "mr", "nbias", "rsum", "rinv"))
        lg = sb("lg", [P, NT, E], F32)
        lmax, lsum, linv = (sb(n, [P, NT], F32) for n in ("lmax", "lsum", "linv"))
        top = sb("top", [P, NT, 8], F32)
        topi = sb("topi", [P, NT, 8], U32)
        eidx = sb("eidx", [P, NT, K], F32)
        oh = sb("oh", [P, K, NT, E], F32)
        picked = sb("picked", [P, NT, E], BF16)
        count = sb("count", [P, E], BF16)
        pos2 = sb("pos2", [P, K, NT, E], F32)
        pos = sb("pos", [P, K, NT], F32)
        slot = sb("slot", [P, K, NT], F32)
        slot_i = sb("slot_i", [P, K, NT], I32)
        hi_i, lo_i = sb("hi_i", [P, K, NT], I32), sb("lo_i", [P, K, NT], I32)
        slot_hi, slot_lo = sb("slot_hi", [P, K, NT], F32), sb("slot_lo", [P, K, NT], F32)
        idw = sb("idw", [P, K, NT], F32)
        gate = sb("gate", [P, K, NT], F32)
        oh_lo = [sb(f"oh_lo{i}", [P, P], F32) for i in range(2)]
        oh_hi = [sb(f"oh_hi{i}", [P, 2 * NSLOT], F32) for i in range(2)]

        s_w, s_small = sem("s_w"), sem("s_small")
        s_wraw = [sem(f"s_wraw{i}") for i in range(3)]
        s_x = [sem("s_x0"), sem("s_x1")]
        s_c = sem("s_c")
        s_const, s_pool = sem("s_const"), sem("s_pool")
        s_bkb, s_init, s_wh, s_whi = sem("s_bkb"), sem("s_init"), sem("s_wh"), sem("s_whi")
        s_y0, s_yT, s_G, s_T, s_M = sem("s_y0"), sem("s_yT"), sem("s_G"), sem("s_T"), sem("s_M")
        s_y1, s_y1h, s_y1l = sem("s_y1"), sem("s_y1h"), sem("s_y1l")
        s_ch, s_cl = sem("s_ch"), sem("s_cl")
        s_vt, s_vh, s_vl = sem("s_vt"), sem("s_vh"), sem("s_vl")
        s_qh, s_ql = sem("s_qh"), sem("s_ql")
        s_nb, s_p, s_ph, s_pl = sem("s_nb"), sem("s_p"), sem("s_ph"), sem("s_pl")
        s_y2, s_base, s_y2T = sem("s_y2"), sem("s_base"), sem("s_y2T")
        s_lg, s_le, s_pick = sem("s_lg"), sem("s_le"), sem("s_pick")
        s_slot, s_oh, s_ohfree = sem("s_slot"), sem("s_oh"), sem("s_ohfree")
        s_out, s_yout = sem("s_out"), sem("s_yout")
        s_zero, s_pad = sem("s_zero"), sem("s_pad")
        s_dve, s_act = sem("s_dve"), sem("s_act")
        s_count, s_cnt = sem("s_count"), sem("s_cnt")

        order = [("INIT", 0)]
        for i in range(-1, B + 1):
            for name, b in (("V", i), ("Y1T", i), ("Y2T", i - 1), ("L", i - 1), ("Q", i), ("X", i - 1),
                            ("LN0", i + 1), ("G", i + 1), ("SC", i), ("Z", i - 1), ("T", i + 1), ("PT", i),
                            ("C", i + 1), ("M", i + 1), ("PV", i), ("A", i + 1)):
                if 0 <= b < B:
                    order.append((name, b))
        block = ctx.enter_context(nc.Block())

        @block.sync
        def _(sp):
            def load_x(b):
                if b >= 2:
                    sp.wait_ge(s_out, 16 * (b - 1))
                sp.dma_start(x[b % 2][:], a["x"][b].rearrange("(t p) d -> p t d", p=P)).then_inc(s_x[b % 2], 16)

            load_x(0)
            sp.dma_start(prob[:], a["WqT"].rearrange("(c p) n -> p c n", p=P)).then_inc(s_wraw[0], 16)
            sp.dma_start(craw[:], a["WkT"].rearrange("(c p) n -> p c n", p=P)).then_inc(s_wraw[1], 16)
            sp.dma_start(y2[:], a["Wv"].rearrange("(c p) n -> p c n", p=P)).then_inc(s_wraw[2], 16)
            for dst, src in ((bias_col[:, 0:NC], a["bq"].rearrange("(c p) -> p c", p=P)),
                             (bias_col[:, NC:2 * NC], a["bk"].rearrange("(c p) -> p c", p=P)),
                             (bv_all[:], a["bv"].partition_broadcast(P)),
                             (rb_all[:], a["rb"].partition_broadcast(P)),
                             (rw[:], a["rw"].rearrange("(c p) e -> p c e", p=P))):
                with nc.allow_non_contiguous_dma(reason="a few columns of biases"):
                    sp.dma_start(dst, src).then_inc(s_small, 16)
            sp.dma_start(CT[:], a["CT"]).then_inc(s_w, 16)
            sp.dma_start(QT[:], a["QT"]).then_inc(s_w, 16)
            load_x(1)
            for name, b in order:
                if name == "C":
                    if b == 0:
                        filled(sp, "QB", 0)
                    else:
                        sp.wait_ge(s_cl, NC * b)
                    sp.dma_start(craw[:], a["ctxT"][b].rearrange("(c p) k -> p c k", p=P)).then_inc(s_c, 16)
                if name == "PV":
                    rows = slice(b * S, (b + 1) * S)
                    sp.wait_ge(s_y2, NT * (b + 1))
                    sp.dma_start(Y[rows, :].rearrange("(t p) d -> p t d", p=P), y2[:]).then_inc(s_yout, 16)
                    sp.wait_ge(s_base, NT * (b + 1))
                    sp.dma_start(out[rows, :].rearrange("(t p) d -> p t d", p=P), x[b % 2][:]).then_inc(s_out, 16)
                    if b + 2 < B:
                        load_x(b + 2)
            sp.wait_ge(s_yout, 16 * B)
            sp.wait_ge(s_out, 16 * B)

        @block.gpsimd
        def _(pool):
            n_pool = [0]

            def link(ins):
                n_pool[0] += 1
                ins.then_inc(s_pool, 1)
                pool.wait_ge(s_pool, n_pool[0])

            link(pool.memset(ident[:], 0.0))
            pool.affine_select(out=ident[:], in_=ident[:], compare_op=ALU.not_equal, fill=1.0, base=0,
                               pattern=[[-1, P]], channel_multiplier=1).then_inc(s_const, 1)
            link(pool.memset(before[:], 1.0))
            pool.affine_select(out=before[:], in_=before[:], compare_op=ALU.is_gt, fill=0.0, base=0,
                               pattern=[[1, P]], channel_multiplier=-1).then_inc(s_const, 1)
            pool.memset(ones[:], 1.0).then_inc(s_const, 1)
            pool.memset(count[:], 0.0).then_inc(s_const, 1)
            pool.memset(slot_list[:], 0.0).then_inc(s_const, 1)
            pool.memset(magic[:], 0x5F3759E0).then_inc(s_const, 1)
            pool.iota(iota_lo[:], [[1, P]], 0, 0, True).then_inc(s_const, 1)
            pool.iota(iota_e[:], [[1, E]], 0, 0, True).then_inc(s_const, 1)
            pool.iota(token_no[:], [[P, B * NT]], 0, 1, True).then_inc(s_const, 1)
            pool.iota(pad_no[:], [[0, E], [P, ET]], N, 1, True).then_inc(s_const, 1)
            pool.memset(vtmp[0][:], 0.0).then_inc(s_zero, 1)
            pool.wait_ge(s_zero, 1)
            for dst in (Y, out):
                pool.dma_start(dst[N:N + PAD, :].rearrange("(t p) d -> p t d", p=P),
                               vtmp[0][:].unsqueeze(1).to_broadcast([P, PAD // P, D])).then_inc(s_pad, 16)
            pool.wait_ge(s_pad, 32)

            for name, b in order:
                if name == "C":
                    if b >= 1:
                        filled(pool, "SC", b - 1, NT - 1)
                    for c in range(NC):
                        pool.wait_ge(s_ch, NC * b + c + 1)
                        pool.tensor_tensor(cl[:, c, :], craw[:, c, :], ch[:, c, :].bitcast(F32),
                                           ALU.subtract).then_inc(s_cl, 1)
                if name == "V":
                    for t in range(NT):
                        pool.wait_ge(s_vh, NT * b + t + 1)
                        pool.tensor_tensor(vl[:, t, :], vtmp[t % 2][:], vh[:, t, :].bitcast(F32),
                                           ALU.subtract).then_inc(s_vl, 1)
                if name == "PV":
                    for t in range(NT):
                        pool.wait_ge(s_y2, NT * b + t + 1)
                        pool.tensor_tensor(x[b % 2][:, t, :], x[b % 2][:, t, :], y2[:, t, :],
                                           ALU.add).then_inc(s_base, 1)
                if name == "Z":
                    pool.wait_ge(s_slot, b + 1)
                    for n in range(K * NT):
                        k, t = divmod(n, NT)
                        m = K * NT * b + n
                        if n >= 2:
                            pool.wait_ge(s_ohfree, (K * NT - 1) * b + n - 1)
                        elif b >= 1 and n == 1:
                            filled(pool, "Z", b - 1)
                        elif b >= 1:
                            pool.wait_ge(s_ohfree, (K * NT - 1) * b)
                        hi = slot_hi[:, k, t:t + 1]
                        pool.tensor_scalar(oh_lo[m % 2][:], iota_lo[:], slot_lo[:, k, t:t + 1], None,
                                           ALU.is_equal).then_inc(s_oh, 1)
                        pool.tensor_scalar(oh_hi[m % 2][:, 0:NSLOT], iota_lo[:, 0:NSLOT], hi,
                                           idw[:, k, t:t + 1], ALU.is_equal, ALU.mult).then_inc(s_oh, 1)
                        pool.tensor_scalar(oh_hi[m % 2][:, NSLOT:2 * NSLOT], iota_lo[:, 0:NSLOT], hi,
                                           gate[:, k, t:t + 1], ALU.is_equal, ALU.mult).then_inc(s_oh, 1)

        @block.scalar
        def _(act):
            def copy(dst, src):
                return act.activation(dst, src, ACT.Copy)

            for name, b in order:
                if name == "INIT":
                    act.wait_ge(s_wraw[2], 16)
                    for c in range(NC):
                        copy(VWH[:, c, :], y2[:, c, :]).then_inc(s_wh, 1)
                    for c in range(NC):
                        filled(act, "W", 0, c)
                        bank = ps[BANK["W"][c]]
                        copy(WH[:, c, :], bank[:]).then_inc(s_whi, 1)
                if name == "Y1T":
                    for c in range(NC):
                        filled(act, "Y1T", b, c)
                        bank = ps[BANK["Y1T"][c]]
                        copy(y1h[:, c, :], bank[:]).then_inc(s_y1h, 1)
                if name == "Y2T":
                    for c in range(NC):
                        filled(act, "Y2T", b, c)
                        bank = ps[BANK["Y2T"][c]]
                        copy(prob[:, c, :], bank[:]).then_inc(s_ev["Y2T"], 1)
                if name == "L":
                    act.wait_ge(s_lg, b + 1)
                    for t in range(NT):
                        act.activation(lg[:, t, :], lg[:, t, :], ACT.Exp, bias=lmax[:, t:t + 1],
                                       accum_out=lsum[:, t:t + 1]).then_inc(s_le, 1)
                if name == "Q":
                    for c in range(NC):
                        filled(act, "Q", b, c)
                        bank = ps[BANK["Q"][c]]
                        act.activation(qh[:, c, :], bank[:], ACT.Identity, bias=qbias[:, 2 * c:2 * c + 1])\
                           .then_inc(s_qh, 1)
                if name == "G":
                    filled(act, "G", b)
                    bank = ps[BANK["G"][0]]
                    copy(G[:], bank[:]).then_inc(s_ev["G"], 1)
                    for c in range(NC):
                        filled(act, "YT", b, c)
                        bank = ps[BANK["YT"][c]]
                        copy(yT[:, c, :], bank[:]).then_inc(s_ev["YT"], 1)
                if name == "SC":
                    for t in range(NT):
                        act.wait_ge(s_nb, NT * b + t + 1)
                        filled(act, "SC", b, t)
                        bank = ps[BANK["SC"][t]]
                        act.activation(prob[:, t, :], bank[:], ACT.Exp, bias=nbias[:, t:t + 1],
                                             scale=SCALE, accum_out=rsum[:, t:t + 1]).then_inc(s_ev["SC"], 1)
                if name == "PT":
                    for c in range(NT):
                        filled(act, "PT", b, c)
                        bank = ps[BANK["PT"][c]]
                        copy(ph[:, c, :], bank[:]).then_inc(s_ph, 1)
                if name == "C":
                    act.wait_ge(s_c, 16 * (b + 1))
                    if b >= 1:
                        filled(act, "SC", b - 1, NT - 1)
                    for c in range(NC):
                        copy(ch[:, c, :], craw[:, c, :]).then_inc(s_ch, 1)
                if name == "V":
                    for t in range(NT):
                        drained(act, "V", b, t)
                        copy(vh[:, t, :], vtmp[t % 2][:]).then_inc(s_vh, 1)

        @block.vector
        def _(dve):
            n_dve = [0]

            def link(ins):
                n_dve[0] += 1
                ins.then_inc(s_dve, 1)
                dve.wait_ge(s_dve, n_dve[0])

            def inverse_deviation():
                link(dve.tensor_scalar(veps[:], mv[:, :, 1], EPS, None, ALU.add))
                link(dve.tensor_scalar(rstd[:].bitcast(I32), veps[:].bitcast(I32), 1, -1,
                                       ALU.logical_shift_right, ALU.bitwise_xor))
                link(dve.tensor_tensor(rstd[:].bitcast(I32), rstd[:].bitcast(I32), magic[:], ALU.add))
                for _ in range(4):
                    link(dve.tensor_tensor(rt[:], rstd[:], rstd[:], ALU.mult))
                    link(dve.scalar_tensor_tensor(rt[:], rt[:], -0.5, veps[:], ALU.mult, ALU.mult))
                    link(dve.scalar_tensor_tensor(rstd[:], rt[:], 1.5, rstd[:], ALU.add, ALU.mult))

            def layer_norm(dst, src, done):
                for t in range(NT):
                    last = dve.bn_stats(stats[:, t, :], src[:, t, :])
                link(last)
                for t in range(NT):
                    last = dve.bn_aggr(mv[:, t, :], stats[:, t, :])
                link(last)
                inverse_deviation()
                for t in range(NT):
                    dve.tensor_scalar(dst[:, t, :], src[:, t, :], mv[:, t, 0:1], rstd[:, t:t + 1],
                                      ALU.subtract, ALU.mult).then_inc(done, 1)

            def minus_hi(dst, bank, hi, key, done):
                ins = dve.tensor_tensor(dst, bank[:], hi.bitcast(F32), ALU.subtract)
                return ins

            dve.wait_ge(s_const, 10)
            for name, b in order:
                if name == "INIT":
                    dve.wait_ge(s_small, 16 * 5)
                    for c in range(NC):
                        last = dve.tensor_copy(M[:, c * P:(c + 1) * P],
                                               bias_col[:, NC + c:NC + c + 1].to_broadcast([P, P]))
                    last.then_inc(s_bkb, 1)
                    for c in range(NC):
                        dve.wait_ge(s_wh, c + 1)
                        last = dve.tensor_tensor(VWL[:, c, :], y2[:, c, :], VWH[:, c, :].bitcast(F32), ALU.subtract)
                    last.then_inc(s_wh, 1)
                    for c in range(NC):
                        dve.wait_ge(s_whi, c + 1)
                        filled(dve, "W", 0, c)
                        bank = ps[BANK["W"][c]]
                        dve.tensor_tensor(WL[:, c, :], bank[:], WH[:, c, :].bitcast(F32), ALU.subtract).then_inc(s_ev["W"], 1)
                    filled(dve, "KR", 0)
                    bank = ps[BANK["KR"][0]]
                    dve.tensor_copy(key_row[:], bank[:]).then_inc(s_ev["KR"], 1)
                    filled(dve, "QB", 0)
                    bank = ps[BANK["QB"][0]]
                    dve.tensor_copy(qbias[:], bank[:, 0:2 * NC + 1]).then_inc(s_ev["QB"], 1)
                    drained(dve, "QB", 0)
                if name == "LN0":
                    dve.wait_ge(s_x[b % 2], 16 * (b // 2 + 1))
                    layer_norm(y, x[b % 2], s_y0)
                if name == "T":
                    for q in range(H):
                        filled(dve, "T", b, q)
                        bank = ps[BANK["T"][q]]
                        dve.tensor_copy(y[:, q, :], bank[:]).then_inc(s_ev["T"], 1)
                if name == "M":
                    filled(dve, "M", b)
                    bank = ps[BANK["M"][0]]
                    dve.tensor_copy(M[:], bank[:]).then_inc(s_ev["M"], 1)
                if name == "A":
                    for t in range(NT):
                        filled(dve, "A", b, t)
                        bank = ps[BANK["A"][t]]
                        dve.tensor_tensor(x[b % 2][:, t, :], bank[:], x[b % 2][:, t, :], ALU.add).then_inc(s_ev["A"], 1)
                    drained(dve, "A", b, NT - 1)
                    layer_norm(y, x[b % 2], s_y1)
                if name == "Y1T":
                    for c in range(NC):
                        dve.wait_ge(s_y1h, NC * b + c + 1)
                        filled(dve, "Y1T", b, c)
                        bank = ps[BANK["Y1T"][c]]
                        dve.tensor_tensor(y1l[:, c, :], bank[:], y1h[:, c, :].bitcast(F32), ALU.subtract).then_inc(s_ev["Y1T"], 1)
                if name == "Q":
                    dve.wait_ge(s_y1, NT * (b + 1))
                    if b >= 1:
                        dve.wait_ge(s_yout, 16 * b)
                        dve.wait_ge(s_base, NT * b)
                        filled(dve, "Y2T", b - 1, NC - 1)
                    for t in range(NT):
                        last = dve.tensor_tensor_reduce(junk[:, t, :], y[:, t, :], key_row[:], 1.0, 0.0,
                                                        ALU.mult, ALU.add, krow[:, t:t + 1])
                    link(last)
                    link(dve.tensor_scalar(krow[:], krow[:], qbias[:, 2 * NC:2 * NC + 1], None, ALU.add))
                    for c in range(NC):
                        dve.wait_ge(s_qh, NC * b + c + 1)
                        filled(dve, "Q", b, c)
                        bank = ps[BANK["Q"][c]]
                        dve.scalar_tensor_tensor(ql[:, c, :], bank[:], qbias[:, 2 * c:2 * c + 1],
                                                       qh[:, c, :].bitcast(F32), ALU.add, ALU.subtract).then_inc(s_ev["Q"], 1)
                if name == "V":
                    for t in range(NT):
                        m = NT * b + t
                        filled(dve, "V", b, t)
                        bank = ps[BANK["V"][t]]
                        if m >= 2:
                            dve.wait_ge(s_vl, m - 1)
                        dve.tensor_tensor(vtmp[t % 2][:], bank[:], bv_all[:], ALU.add).then_inc(s_ev["V"], 1)
                if name == "SC":
                    for t in range(NT):
                        filled(dve, "SC", b, t)
                        bank = ps[BANK["SC"][t]]
                        link(dve.reduce_max(smax[:, t:t + 1], bank[:], AX_X))
                        link(dve.tensor_tensor(mr[:, t:t + 1], smax[:, t:t + 1], krow[:, t:t + 1], ALU.add))
                        dve.tensor_scalar(nbias[:, t:t + 1], mr[:, t:t + 1], krow[:, t:t + 1], -SCALE,
                                          ALU.subtract, ALU.mult).then_inc(s_nb, 1)
                if name == "PT":
                    for c in range(NT):
                        dve.wait_ge(s_ph, NT * b + c + 1)
                        filled(dve, "PT", b, c)
                        bank = ps[BANK["PT"][c]]
                        dve.tensor_tensor(pl[:, c, :], bank[:], ph[:, c, :].bitcast(F32), ALU.subtract).then_inc(s_ev["PT"], 1)
                if name == "PV":
                    drained(dve, "SC", b, NT - 1)
                    link(dve.reciprocal(rinv[:], rsum[:]))
                    for t in range(NT):
                        filled(dve, "PV", b, t)
                        bank = ps[BANK["PV"][t]]
                        dve.scalar_tensor_tensor(x[b % 2][:, t, :], bank[:], rinv[:, t:t + 1],
                                                       x[b % 2][:, t, :], ALU.mult, ALU.add).then_inc(s_ev["PV"], 1)
                    drained(dve, "PV", b, NT - 1)
                    layer_norm(y2, x[b % 2], s_y2)
                if name == "L":
                    filled(dve, "L", b)
                    bank = ps[BANK["L"][0]]
                    dve.tensor_tensor(lg[:], bank[:, 0:NT * E].rearrange("p (t e) -> p t e", e=E),
                                            rb_all[:].unsqueeze(1).to_broadcast([P, NT, E]), ALU.add).then_inc(s_ev["L"], 1)
                    drained(dve, "L", b)
                    dve.tensor_reduce(lmax[:], lg[:], AX_X, ALU.max, negate=True).then_inc(s_lg, 1)
                    dve.wait_ge(s_le, NT * (b + 1))
                    link(dve.reciprocal(linv[:], lsum[:]))
                    link(dve.tensor_tensor(lg[:], lg[:], linv[:].unsqueeze(2).to_broadcast([P, NT, E]), ALU.mult))
                    for t in range(NT):
                        last = dve.max(top[:, t, :], lg[:, t, :])
                    link(last)
                    for t in range(NT):
                        last = dve.max_index(topi[:, t, :], top[:, t, :], lg[:, t, :])
                    link(last)
                    link(dve.tensor_copy(eidx[:], topi[:, :, 0:K]))
                    for k in range(K):
                        last = dve.tensor_tensor(oh[:, k], iota_e[:].unsqueeze(1).to_broadcast([P, NT, E]),
                                                 eidx[:, :, k:k + 1].to_broadcast([P, NT, E]), ALU.is_equal)
                    link(last)
                    dve.tensor_tensor(picked[:], oh[:, 0], oh[:, 1], ALU.add).then_inc(s_pick, 1)
                    link(dve.tensor_tensor(linv[:], top[:, :, 0], top[:, :, 1], ALU.add))
                    link(dve.tensor_scalar(linv[:], linv[:], 1e-9, None, ALU.add))
                    link(dve.reciprocal(linv[:], linv[:]))
                    if b >= 1:
                        dve.wait_ge(s_oh, 3 * K * NT * b)
                    for k in range(K):
                        dve.tensor_tensor(gate[:, k, :], top[:, :, k], linv[:], ALU.mult).then_inc(s_count, 1)
                if name == "X":
                    filled(dve, "X", b)
                    bank = ps[BANK["X"][0]]
                    for k in range(K):
                        last = dve.tensor_tensor(pos2[:, k], bank[:, 0:NT * E].rearrange("p (t e) -> p t e", e=E),
                                                 oh[:, k], ALU.mult)
                    last.then_inc(s_ev["X"], 1)
                    drained(dve, "X", b)
                    link(dve.tensor_reduce(pos[:], pos2[:], AX_X, ALU.add))
                    link(dve.tensor_scalar(slot[:], pos[:], float(CAP), float(1 << 16), ALU.is_ge, ALU.mult))
                    link(dve.tensor_tensor(slot[:], slot[:], pos[:], ALU.add))
                    for k in range(K):
                        last = dve.scalar_tensor_tensor(slot[:, k], eidx[:, :, k], float(CAP), slot[:, k],
                                                        ALU.mult, ALU.add)
                    link(last)
                    link(dve.tensor_copy(slot_i[:], slot[:]))
                    dve.tensor_scalar(lo_i[:], slot_i[:], P - 1, None, ALU.bitwise_and)
                    link(dve.tensor_scalar(hi_i[:], slot_i[:], 7, None, ALU.logical_shift_right))
                    dve.tensor_copy(slot_lo[:], lo_i[:]).then_inc(s_count, 1)
                    dve.tensor_copy(slot_hi[:], hi_i[:]).then_inc(s_count, 1)
                    for k in range(K):
                        last = dve.scalar_tensor_tensor(idw[:, k], pos[:, k], -1.0,
                                                        token_no[:, b * NT:(b + 1) * NT], ALU.mult, ALU.add)
                    link(last)
                    dve.wait_ge(s_count, 4 * (b + 1))
                    dve.tensor_scalar(idw[:], idw[:], -float(N), None, ALU.add).then_inc(s_slot, 1)
                    for t in range(NT):
                        last = dve.tensor_tensor(count[:], count[:], picked[:, t, :], ALU.add)
                        if t < NT - 1:
                            link(last)
                    last.then_inc(s_cnt, 1)
                    dve.wait_ge(s_cnt, b + 1)
                if name == "Z":
                    filled(dve, "Z", b)
                    bank = ps[BANK["Z"][0]]
                    dve.tensor_tensor(slot_list[:], bank[:, 0:2 * NSLOT], slot_list[:], ALU.add).then_inc(s_ev["Z"], 1)
                    drained(dve, "Z", b)
            dve.tensor_tensor(slot_index[:], slot_list[:, 0:NSLOT], pad_no[:], ALU.add).then_inc(s_dve, 1)

        @block.tensor
        def _(pe):
            def f32_group(out, pairs):
                for i, (left, right) in enumerate(pairs):
                    last = pe.matmul(out, left, right, start=(i == 0), stop=(i == len(pairs) - 1))
                return last

            def transposes(step, src, c):
                for t in range(NT):
                    last = pe.transpose(ps[BANK[step][c]][:, t * P:(t + 1) * P], src[:, t, c * P:(c + 1) * P],
                                        ident[:])
                last.then_inc(s_mm[step], 1)

            pe.wait_ge(s_const, 10)
            for name, b in order:
                if name == "INIT":
                    pe.wait_ge(s_wraw[0], 16)
                    pe.wait_ge(s_wraw[1], 16)
                    for c in range(NC):
                        f32_group(ps[BANK["W"][c]][:], [(prob[:, j, c * P:(c + 1) * P], craw[:, j, :])
                                                        for j in range(NC)]).then_inc(s_mm["W"], 1)
                    pe.wait_ge(s_bkb, 1)
                    pe.wait_ge(s_small, 16 * 5)
                    f32_group(ps[BANK["KR"][0]][:], [(M[:, j * P:(j + 1) * P], prob[:, j, :])
                                                     for j in range(NC)]).then_inc(s_mm["KR"], 1)
                    bank = ps[BANK["QB"][0]]
                    for c in range(NC):
                        f32_group(bank[:, 2 * c:2 * c + 2],
                                  [(craw[:, j, c * P:(c + 1) * P], bias_col[:, j:j + 2]) for j in range(NC)])
                    f32_group(bank[:, 2 * NC:2 * NC + 1], [(M[:, j * P:(j + 1) * P], bias_col[:, j:j + 1])
                                                           for j in range(NC)]).then_inc(s_mm["QB"], 1)
                    pe.wait_ge(s_ev["W"], NC)
                    pe.wait_ge(s_ev["KR"], 1)
                    pe.wait_ge(s_ev["QB"], 1)
                if name == "V":
                    if b == 0:
                        pe.wait_ge(s_wh, NC + 1)
                    pe.wait_ge(s_cl, NC * (b + 1))
                    drained(pe, "PV", b - 1, 3)
                    for t in range(NT):
                        if t > 0:
                            drained(pe, "A", b, t - 1)
                        cols = slice(t * P, (t + 1) * P)
                        three_pass(pe, ps[BANK["V"][t]][:], [(ch[:, c, cols], cl[:, c, cols], VWH[:, c, :], VWL[:, c, :])
                                                             for c in range(NC)]).then_inc(s_mm["V"], 1)
                if name == "Y1T":
                    pe.wait_ge(s_y1, NT * (b + 1))
                    drained(pe, "PV", b - 1, 2)
                    for c in range(NC):
                        transposes("Y1T", y, c)
                if name == "Y2T":
                    pe.wait_ge(s_y2, NT * (b + 1))
                    for c in range(NC):
                        drained(pe, "V", b + 1, c)
                        transposes("Y2T", y2, c)
                if name == "L":
                    drained(pe, "Y2T", b, NC - 1)
                    drained(pe, "Y1T", b + 1, 0)
                    for t in range(NT):
                        last = f32_group(ps[BANK["L"][0]][:, t * E:(t + 1) * E],
                                         [(prob[:, c, t * P:(t + 1) * P], rw[:, c, :]) for c in range(NC)])
                    last.then_inc(s_mm["L"], 1)
                if name == "Q":
                    drained(pe, "Y1T", b, NC - 1)
                    drained(pe, "Y2T", b - 1, 0)
                    if b == 0:
                        drained(pe, "V", 0, NT - 1)
                    for c in range(NC):
                        cols = slice(c * P, (c + 1) * P)
                        three_pass(pe, ps[BANK["Q"][c]][:], [(WH[:, j, cols], WL[:, j, cols], y1h[:, j, :], y1l[:, j, :])
                                                             for j in range(NC)]).then_inc(s_mm["Q"], 1)
                if name == "X":
                    pe.wait_ge(s_pick, b + 1)
                    pe.wait_ge(s_cnt, b)
                    for t in range(NT):
                        pairs = [(before[:], picked[:, t, :])] + [(ones[:], picked[:, i, :]) for i in range(t)]
                        last = f32_group(ps[BANK["X"][0]][:, t * E:(t + 1) * E], pairs + [(ones[:], count[:])])
                    last.then_inc(s_mm["X"], 1)
                if name == "G":
                    pe.wait_ge(s_y0, NT * (b + 1))
                    drained(pe, "Y2T", b - 2, 3)
                    for q in range(H):
                        cols = slice(q * P, (q + 1) * P)
                        last = f32_group(ps[BANK["G"][0]][:, cols], [(y[:, t, cols], y[:, t, cols]) for t in range(NT)])
                    last.then_inc(s_mm["G"], 1)
                    drained(pe, "L", b - 2)
                    drained(pe, "Q", b - 1, 1)
                    for c in range(NC):
                        transposes("YT", y, c)
                if name == "SC":
                    drained(pe, "Q", b, NC - 1)
                    drained(pe, "X", b - 1)
                    drained(pe, "G", b + 1)
                    for t in range(NT):
                        cols = slice(t * P, (t + 1) * P)
                        three_pass(pe, ps[BANK["SC"][t]][:], [(qh[:, c, cols], ql[:, c, cols], ch[:, c, :], cl[:, c, :])
                                                              for c in range(NC)]).then_inc(s_mm["SC"], 1)
                if name == "Z":
                    drained(pe, "YT", b + 2, 0)
                    for n in range(K * NT):
                        m = K * NT * b + n
                        pe.wait_ge(s_oh, 3 * (m + 1))
                        last = pe.matmul(ps[BANK["Z"][0]][:, 0:2 * NSLOT], oh_lo[m % 2][:], oh_hi[m % 2][:],
                                         start=(n == 0), stop=(n == K * NT - 1))
                        last.then_inc(s_ohfree if n < K * NT - 1 else s_mm["Z"], 1)
                if name == "T":
                    if b == 0:
                        pe.wait_ge(s_w, 32)
                    drained(pe, "G", b)
                    drained(pe, "YT", b, 3)
                    drained(pe, "SC", b - 1, 0)
                    for q in range(H):
                        pe.matmul(ps[BANK["T"][q]][:], G[:, q * P:(q + 1) * P], CT[:, q, :],
                                  start=True, stop=True).then_inc(s_mm["T"], 1)
                if name == "PT":
                    drained(pe, "SC", b, NT - 1)
                    drained(pe, "Z", b - 1)
                    drained(pe, "YT", b + 1, 0)
                    for c in range(NT):
                        transposes("PT", prob, c)
                if name == "M":
                    drained(pe, "T", b, H - 1)
                    for h in range(H):
                        cols = slice(h * P, (h + 1) * P)
                        last = f32_group(ps[BANK["M"][0]][:, cols], [(QT[:, h, q, :], y[:, q, cols]) for q in range(H)])
                    last.then_inc(s_mm["M"], 1)
                if name == "PV":
                    drained(pe, "PT", b, NT - 1)
                    pe.wait_ge(s_vl, NT * (b + 1))
                    drained(pe, "T", b + 1, 3)
                    for t in range(NT):
                        cols = slice(t * P, (t + 1) * P)
                        three_pass(pe, ps[BANK["PV"][t]][:], [(ph[:, c, cols], pl[:, c, cols], vh[:, c, :], vl[:, c, :])
                                                              for c in range(NT)]).then_inc(s_mm["PV"], 1)
                if name == "A":
                    drained(pe, "M", b)
                    drained(pe, "YT", b, NC - 1)
                    drained(pe, "PT", b - 1, 3)
                    for t in range(NT):
                        for h in range(H):
                            cols = slice(h * P, (h + 1) * P)
                            last = pe.matmul(ps[BANK["A"][t]][:, cols], yT[:, h, t * P:(t + 1) * P], M[:, cols],
                                             start=True, stop=True)
                        last.then_inc(s_mm["A"], 1)


def phase2(nc, a, Y, shared):
    out = a["out"]
    ident, slot_list, slot_index = shared["ident"], shared["slot_list"], shared["slot_index"]
    RING = 22
    RAW = 6
    TMP = 3
    with ExitStack() as ctx:
        def sb(name, shape, dt):
            return ctx.enter_context(nc.sbuf_tensor(name, shape, dt))

        def sem(name):
            return ctx.enter_context(nc.semaphore(name))

        ps = [ctx.enter_context(nc.psum_tensor(f"ps_m{i}", [P, 512], F32)) for i in range(BANKS)]
        gate_bank = [ps[0], ps[2]]
        up_bank = [ps[1], ps[3]]
        down_bank = [ps[4], ps[5]]
        x_bank = [ps[6], ps[7]]
        wraw = [sb(f"wraw{i}", [P, D], F32) for i in range(RAW)]
        wh = [sb(f"wh{i}", [P, D], F32R) for i in range(RING)]
        wl = [sb(f"wl{i}", [P, D], F32R) for i in range(RING)]
        xn = [sb(f"xn{i}", [P, ET, D], F32) for i in range(2)]
        xh, xl = sb("xh", [P, NC, CAP], F32R), sb("xl", [P, NC, CAP], F32R)
        hh, hl = sb("hh", [P, FC, CAP], F32R), sb("hl", [P, FC, CAP], F32R)
        silu = [sb(f"silu{i}", [P, 512], F32) for i in range(TMP)]
        ht = [sb(f"ht{i}", [P, 512], F32) for i in range(TMP)]
        ost = sb("ost", [P, ET, D], F32)

        s_zero, s_raw = sem("t_zero"), [sem(f"t_raw{i}") for i in range(RAW)]
        s_wh, s_wl = sem("t_wh"), sem("t_wl")
        s_xn = [sem("t_xn0"), sem("t_xn1")]
        s_xg = [sem("t_xg0"), sem("t_xg1")]
        s_xT, s_xh, s_xl = sem("t_xT"), sem("t_xh"), sem("t_xl")
        s_gu, s_silu, s_ht, s_hh, s_hl = sem("t_gu"), sem("t_silu"), sem("t_ht"), sem("t_hh"), sem("t_hl")
        s_down, s_ost = sem("t_down"), sem("t_ost")
        s_add = [sem(f"t_add{i}") for i in range(ET)]

        groups = [(0, g, NT, g == B - 1) for g in range(B)] + [(1 + e, e, ET, True) for e in range(E)]
        NG = len(groups)
        tiles_of = [tiles for _, _, tiles, _ in groups]
        tiles_before = [sum(tiles_of[:g]) for g in range(NG + 1)]

        def cuts(g):
            n = tiles_of[g] * P
            return [(0, n)] if n <= 512 else [(0, n // 2), (n // 2, n // 2)]

        units = [(g, c, j) for g in range(NG) for c in range(FC) for j in range(len(cuts(g)))]
        unit_no = {u: n for n, u in enumerate(units)}
        n_chunks = (1 + E) * WC
        FIRST = 4
        EACH = -(-(RING - FIRST) // FC)

        def split_after(g, step):
            job, _, _, last = groups[g]
            if g == 0 and step != "down":
                return list(range(FIRST + step * EACH, min(FIRST + (step + 1) * EACH, RING)))
            if not last:
                return []
            done = range(GU, WC) if step == "down" else range(2 * step, min(2 * step + 2, GU))
            return [job * WC + i + RING for i in done if job * WC + i + RING < n_chunks]

        def wait_last_use(eng, n):
            job, i = divmod(n, WC)
            g = B - 1 + job
            if i < GU:
                eng.wait_ge(s_gu, unit_no[(g, i // 2, len(cuts(g)) - 1)] + 1)
            else:
                eng.wait_ge(s_down, tiles_before[g + 1])

        def adds_of(g, t):
            return sum(tiles > t for tiles in tiles_of[:g])

        def rows_of(c):
            return P if c < FC - 1 else FH

        def tail(g):
            after = tiles_of[g + 1] if g + 1 < NG else 0
            for t in range(max(tiles_of[g], after)):
                if t < after:
                    yield "x", g + 1, t
                if t < tiles_of[g]:
                    yield "down", g, t

        block = ctx.enter_context(nc.Block())

        @block.sync
        def _(sp):
            def load_tokens(g):
                if g >= 2:
                    sp.wait_ge(s_xT, tiles_before[g - 1])
                sp.dma_start(xn[g % 2][:, 0:NT, :], Y[g * S:(g + 1) * S, :].rearrange("(t p) d -> p t d", p=P))\
                  .then_inc(s_xn[g % 2], 16)

            load_tokens(0)
            for n in range(n_chunks):
                if n >= RAW:
                    sp.wait_ge(s_wl, n - RAW + 1)
                job, i = divmod(n, WC)
                sp.dma_start(wraw[n % RAW][:], a["wts"][job, :, i * D:(i + 1) * D]).then_inc(s_raw[n % RAW], 16)
                if n == RING - 1:
                    for g in range(1, B):
                        load_tokens(g)

        @block.gpsimd
        def _(pool):
            def split(n):
                pool.wait_ge(s_wh, n + 1)
                pool.tensor_tensor(wl[n % RING][:], wraw[n % RAW][:], wh[n % RING][:].bitcast(F32),
                                   ALU.subtract).then_inc(s_wl, 1)

            def slots(e, t):
                return bass.IndirectOffsetOnAxis(ap=slot_index[:, e * ET + t:e * ET + t + 1], axis=0)

            def gather(g):
                pool.wait_ge(s_xT, tiles_before[g - 1])
                for t in range(ET):
                    pool.indirect_dma_start(xn[g % 2][:, t, :], None, Y[:, :], slots(groups[g][1], t),
                                            bounds_check=N + PAD - 1).then_inc(s_xg[g % 2], 16)

            for n in range(FIRST):
                split(n)
            for g, (job, part, tiles, last) in enumerate(groups):
                if g + 1 < NG and groups[g + 1][0] > 0:
                    gather(g + 1)
                for c in range(FC):
                    for n in split_after(g, c):
                        split(n)
                for t in range(tiles):
                    pool.wait_ge(s_ost, tiles_before[g] + t + 1)
                    if job == 0:
                        pool.dma_start(out[part * S + t * P:part * S + (t + 1) * P, :], ost[:, t, :],
                                       accum_op=ALU.add).then_inc(s_add[t], 16)
                        continue
                    if t == 0:
                        for i in range(ET):
                            pool.wait_ge(s_add[i], 16 * adds_of(g, i))
                    pool.indirect_dma_start(out[:, :], slots(part, t), ost[:, t, :], None,
                                            bounds_check=N + PAD - 1, compute_op=ALU.add).then_inc(s_add[t], 16)
                for n in split_after(g, "down"):
                    split(n)
            for i in range(ET):
                pool.wait_ge(s_add[i], 16 * adds_of(NG, i))

        @block.scalar
        def _(act):
            def copy(dst, src):
                return act.activation(dst, src, ACT.Copy)

            def split(n):
                act.wait_ge(s_raw[n % RAW], 16 * (n // RAW + 1))
                if n >= RING:
                    wait_last_use(act, n - RING)
                copy(wh[n % RING][:], wraw[n % RAW][:]).then_inc(s_wh, 1)

            def x_hi(g, t):
                n = tiles_before[g] + t
                act.wait_ge(s_xT, n + 1)
                copy(xh[:, :, t * P:(t + 1) * P], x_bank[n % 2][:].rearrange("p (c n) -> p c n", c=NC))\
                    .then_inc(s_xh, 1)

            def h_hi(u):
                g, c, j = units[u]
                first, n = cuts(g)[j]
                act.wait_ge(s_ht, u + 1)
                copy(hh[0:rows_of(c), c, first:first + n], ht[u % TMP][0:rows_of(c), 0:n]).then_inc(s_hh, 1)

            for t in range(NT):
                x_hi(0, t)
            for n in range(FIRST):
                split(n)
            for g in range(NG):
                for c in range(FC):
                    for j, (first, n) in enumerate(cuts(g)):
                        u = unit_no[(g, c, j)]
                        if u >= TMP:
                            act.wait_ge(s_ht, u - TMP + 1)
                        act.wait_ge(s_gu, u + 1)
                        bank = gate_bank[u % 2] if c < FC - 1 else up_bank[u % 2]
                        act.activation(silu[u % TMP][0:rows_of(c), 0:n], bank[0:rows_of(c), 0:n], ACT.Silu)\
                           .then_inc(s_silu, 1)
                        if u > unit_no[(g, 0, 0)]:
                            h_hi(u - 1)
                    if c > 0:
                        for m in split_after(g, c - 1):
                            split(m)
                h_hi(u)
                for m in split_after(g, FC - 1):
                    split(m)
                for what, gx, t in tail(g):
                    if what == "x":
                        x_hi(gx, t)
                for m in split_after(g, "down"):
                    split(m)

        @block.vector
        def _(dve):
            def x_lo(g, t):
                n = tiles_before[g] + t
                dve.wait_ge(s_xh, n + 1)
                cols = slice(t * P, (t + 1) * P)
                dve.tensor_tensor(xl[:, :, cols], x_bank[n % 2][:].rearrange("p (c n) -> p c n", c=NC),
                                  xh[:, :, cols].bitcast(F32), ALU.subtract).then_inc(s_xl, 1)

            def h_lo(u):
                g, c, j = units[u]
                first, n = cuts(g)[j]
                rows = rows_of(c)
                dve.wait_ge(s_hh, u + 1)
                dve.tensor_tensor(hl[0:rows, c, first:first + n], ht[u % TMP][0:rows, 0:n],
                                  hh[0:rows, c, first:first + n].bitcast(F32), ALU.subtract).then_inc(s_hl, 1)

            dve.memset(hh[FH:P, FC - 1, :].bitcast(F32), 0.0).then_inc(s_zero, 1)
            dve.memset(hl[FH:P, FC - 1, :].bitcast(F32), 0.0).then_inc(s_zero, 1)
            for t in range(NT):
                x_lo(0, t)
            for g, (job, part, _, _) in enumerate(groups):
                for c in range(FC):
                    for j, (first, n) in enumerate(cuts(g)):
                        u = unit_no[(g, c, j)]
                        if u >= TMP:
                            dve.wait_ge(s_hl, u - TMP + 1)
                        dve.wait_ge(s_silu, u + 1)
                        rows = slice(0, P) if c < FC - 1 else slice(FH, 2 * FH)
                        dve.tensor_tensor(ht[u % TMP][0:rows_of(c), 0:n], up_bank[u % 2][rows, 0:n],
                                          silu[u % TMP][0:rows_of(c), 0:n], ALU.mult).then_inc(s_ht, 1)
                        if u > unit_no[(g, 0, 0)]:
                            h_lo(u - 1)
                h_lo(u)
                for what, gx, t in tail(g):
                    if what == "x":
                        x_lo(gx, t)
                        continue
                    n = tiles_before[g] + t
                    dve.wait_ge(s_down, n + 1)
                    if adds_of(g, t):
                        dve.wait_ge(s_add[t], 16 * adds_of(g, t))
                    if job == 0:
                        dve.tensor_copy(ost[:, t, :], down_bank[n % 2][:]).then_inc(s_ost, 1)
                    else:
                        gate = NSLOT + part * ET + t
                        dve.tensor_scalar(ost[:, t, :], down_bank[n % 2][:], slot_list[:, gate:gate + 1], None,
                                          ALU.mult).then_inc(s_ost, 1)

        @block.tensor
        def _(pe):
            def transpose_tile(g, t):
                n = tiles_before[g] + t
                if t == 0 and groups[g][0] == 0:
                    pe.wait_ge(s_xn[g % 2], 16 * (g // 2 + 1))
                if groups[g][0] > 0:
                    pe.wait_ge(s_xg[g % 2], 16 * ET * ((g - B) // 2 + 1))
                if n >= 2:
                    pe.wait_ge(s_xl, n - 1)
                for c in range(NC):
                    ins = pe.transpose(x_bank[n % 2][:, c * P:(c + 1) * P], xn[g % 2][:, t, c * P:(c + 1) * P],
                                       ident[:])
                ins.then_inc(s_xT, 1)

            pe.wait_ge(s_zero, 2)
            for t in range(NT):
                transpose_tile(0, t)
            for g, (job, _, tiles, _) in enumerate(groups):
                base = job * WC
                pe.wait_ge(s_xl, tiles_before[g + 1])
                for c in range(FC):
                    for j, (first, n) in enumerate(cuts(g)):
                        u = unit_no[(g, c, j)]
                        if u >= 2:
                            pe.wait_ge(s_ht, u - 1)
                        cols = slice(first, first + n)
                        chunks = ([(gate_bank, 2 * c)] if c < FC - 1 else []) + [(up_bank, min(2 * c + 1, GU - 1))]
                        for bank, i in chunks:
                            m = base + i
                            pe.wait_ge(s_wl, m + 1)
                            ins = three_pass(pe, bank[u % 2][:, 0:n], [
                                (wh[m % RING][:, d * P:(d + 1) * P], wl[m % RING][:, d * P:(d + 1) * P],
                                 xh[:, d, cols], xl[:, d, cols]) for d in range(NC)])
                        ins.then_inc(s_gu, 1)
                for what, gx, t in tail(g):
                    if what == "x":
                        transpose_tile(gx, t)
                        continue
                    n = tiles_before[g] + t
                    if n >= 2:
                        pe.wait_ge(s_ost, n - 1)
                    cols = slice(t * P, (t + 1) * P)
                    for c in range(FC):
                        m = base + GU + c
                        if t == 0:
                            pe.wait_ge(s_wl, m + 1)
                            pe.wait_ge(s_hl, unit_no[(g, c, len(cuts(g)) - 1)] + 1)
                        for i, (left, right) in enumerate(((hh, wh), (hh, wl), (hl, wh))):
                            ins = pe.matmul(down_bank[n % 2][:], left[:, c, cols], right[m % RING][:],
                                            start=(c == 0 and i == 0), stop=(c == FC - 1 and i == 2))
                    ins.then_inc(s_down, 1)


def kernel(x, ctx_1024, L0_attn_queries, L0_attn_combiners, L0_xattn_Wq, L0_xattn_bq, L0_xattn_Wk, L0_xattn_bk,
           L0_xattn_Wv, L0_xattn_bv, L0_ffn_router_w, L0_ffn_router_b, L0_ffn_w_gate, L0_ffn_w_up, L0_ffn_w_down,
           L0_ffn_sw_gate, L0_ffn_sw_up, L0_ffn_sw_down):
    import numpy as np
    import concourse.bacc as bacc
    from concourse.bass_utils import run_bass_kernel_spmd

    def chunks(gate, up, down):
        j = gate.shape[0]
        full = (FC - 1) * P
        g = gate.reshape(j, NC, P, F)
        u = up.reshape(j, NC, P, F)
        pairs = np.stack([g[..., :full].reshape(j, NC, P, FC - 1, P), u[..., :full].reshape(j, NC, P, FC - 1, P)], 4)
        pairs = pairs.transpose(0, 2, 3, 4, 1, 5).reshape(j, P, (GU - 1) * D)
        mixed = np.concatenate([g[..., full:], u[..., full:]], 3).transpose(0, 2, 1, 3).reshape(j, P, D)
        d = np.pad(down, ((0, 0), (0, FC * P - F), (0, 0))).reshape(j, FC, P, D).transpose(0, 2, 1, 3)
        return np.concatenate([pairs, mixed, d.reshape(j, P, FC * D)], 2)

    q = np.asarray(L0_attn_queries).reshape(H, P, H, P)
    c = np.asarray(L0_attn_combiners).reshape(H, H, P, P)
    gate, up, down, sgate, sup, sdown = (np.asarray(w) for w in (
        L0_ffn_w_gate, L0_ffn_w_up, L0_ffn_w_down, L0_ffn_sw_gate, L0_ffn_sw_up, L0_ffn_sw_down))
    arrays = {
        "x": np.asarray(x),
        "ctxT": np.ascontiguousarray(np.asarray(ctx_1024).transpose(0, 2, 1)),
        "QT": np.ascontiguousarray(q.transpose(3, 0, 2, 1)),
        "CT": np.ascontiguousarray(c.transpose(2, 1, 0, 3)).reshape(P, H, H * P),
        "WqT": np.ascontiguousarray(np.asarray(L0_xattn_Wq).T),
        "WkT": np.ascontiguousarray(np.asarray(L0_xattn_Wk).T),
        "Wv": np.asarray(L0_xattn_Wv),
        "bq": np.asarray(L0_xattn_bq), "bk": np.asarray(L0_xattn_bk), "bv": np.asarray(L0_xattn_bv),
        "rw": np.asarray(L0_ffn_router_w), "rb": np.asarray(L0_ffn_router_b),
        "wts": np.concatenate([chunks(sgate[None], sup[None], sdown[None]), chunks(gate, up, down)], 0),
    }
    nc = bacc.Bacc("TRN2", target_bir_lowering=False, num_devices=1)
    args = {k: nc.dram_tensor(f"in_{k}", v.shape, F32, kind="ExternalInput").ap() for k, v in arrays.items()}
    args["out"] = nc.dram_tensor("out_tokens", (N + PAD, D), F32, kind="ExternalOutput").ap()
    build(nc, args)
    r = run_bass_kernel_spmd(nc, [{f"in_{k}": v for k, v in arrays.items()}], core_ids=[0])
    return r.results[0]["out_tokens"][:N].reshape(B, S, D)
```

```python
from contextlib import ExitStack

import concourse.bass as bass
from concourse import mybir

F32 = mybir.dt.float32
F32R = mybir.dt.float32r
BF16 = mybir.dt.bfloat16
I32 = mybir.dt.int32
U32 = mybir.dt.uint32
ALU = mybir.AluOpType
ACT = mybir.ActivationFunctionType
AX_X = mybir.AxisListType.X

P = 128
B, S, D = 8, 512, 512
NT = S // P
NC = D // P
H = NC
N = B * S
E, K, F = 16, 2, 704
CAP = -(-5 * N * K // (4 * E))
ET = CAP // P
NSLOT = E * ET
FC = -(-F // P)
FH = F - (FC - 1) * P
GU = 2 * (FC - 1) + 1
WC = GU + FC
PAD = CAP
EPS = 1e-5
SCALE = float(D) ** -0.5
BANKS = 8
XS = 3
OS = 4


def three_pass(pe, out, parts):
    last = None
    todo = []
    for lh, ll, rh, rl in parts:
        todo += [(lh, rh), (lh, rl), (ll, rh)]
    for i, (left, right) in enumerate(todo):
        last = pe.matmul(out, left, right, start=(i == 0), stop=(i == len(todo) - 1))
    return last


def build(nc, a):
    Y = nc.dram_tensor("tokens_normed", (N + PAD, D), F32, kind="Internal").ap()
    with ExitStack() as keep:
        def sb(name, shape, dt):
            return keep.enter_context(nc.sbuf_tensor(name, shape, dt))

        shared = {
            "ident": sb("ident", [P, P], F32),
            "slot_list": sb("slot_list", [P, 2 * NSLOT], F32),
            "slot_index": sb("slot_index", [P, NSLOT], U32),
        }
        phase1(nc, a, Y, shared)
        phase2(nc, a, Y, shared)


def phase1(nc, a, Y, shared):
    out = a["out"]
    ident, slot_list, slot_index = shared["ident"], shared["slot_list"], shared["slot_index"]
    with ExitStack() as ctx:
        def sb(name, shape, dt):
            return ctx.enter_context(nc.sbuf_tensor(name, shape, dt))

        def sem(name):
            return ctx.enter_context(nc.semaphore(name))

        ps = [ctx.enter_context(nc.psum_tensor(f"ps_a{i}", [P, 512], F32)) for i in range(BANKS)]
        BANK = {"Y1T": (0, 1, 2, 3), "V": (4, 5, 6, 7), "Y2T": (0, 1, 2, 3), "Q": (4, 5, 6, 7), "G": (0,),
                "YT": (1, 2, 3, 4), "L": (5,), "SC": (6, 7, 0, 1), "T": (2, 3, 4, 5), "X": (6,),
                "PT": (7, 0, 1, 2), "M": (3,), "Z": (4,), "A": (5, 6, 7, 0), "PV": (1, 2, 3, 4),
                "W": (5, 6, 7, 0), "KR": (1,), "QB": (2,)}
        s_mm = {k: ctx.enter_context(nc.semaphore(f"s_mm_{k}")) for k in BANK}
        s_ev = {k: ctx.enter_context(nc.semaphore(f"s_ev_{k}")) for k in BANK}

        def filled(eng, step, b, i=0):
            eng.wait_ge(s_mm[step], len(BANK[step]) * b + i + 1)

        def drained(eng, step, b, i=0):
            if 0 <= b < B:
                eng.wait_ge(s_ev[step], len(BANK[step]) * b + i + 1)

        WH, WL = sb("WH", [P, NC, D], F32R), sb("WL", [P, NC, D], F32R)
        VWH, VWL = sb("VWH", [P, NC, D], F32R), sb("VWL", [P, NC, D], F32R)
        QT = sb("QT", [P, H, H, P], F32)
        CT = sb("CT", [P, H, H * P], F32)
        bv_all = sb("bv_all", [P, D], F32)
        key_row = sb("key_row", [P, D], F32)
        rw = sb("rw", [P, NC, E], F32)
        rb_all = sb("rb_all", [P, E], F32)
        bias_col = sb("bias_col", [P, 2 * NC], F32)
        qbias = sb("qbias", [P, 2 * NC + 1], F32)
        before = sb("before", [P, P], BF16)
        ones = sb("ones", [P, P], BF16)
        iota_lo = sb("iota_lo", [P, P], F32)
        iota_e = sb("iota_e", [P, E], F32)
        token_no = sb("token_no", [P, B * NT], F32)
        pad_no = sb("pad_no", [P, NSLOT], F32)
        magic = sb("magic", [P, NT], I32)
        x = [sb(f"x{i}", [P, NT, D], F32) for i in range(XS)]
        y = sb("y", [P, NT, D], F32)
        yT = sb("yT", [P, NC, S], F32)
        G = sb("G", [P, H * P], F32)
        M = sb("M", [P, H * P], F32)
        y1h, y1l = sb("y1h", [P, NC, S], F32R), sb("y1l", [P, NC, S], F32R)
        qh, ql = sb("qh", [P, NC, S], F32R), sb("ql", [P, NC, S], F32R)
        craw = sb("craw", [P, NC, S], F32)
        ch, cl = sb("ch", [P, NC, S], F32R), sb("cl", [P, NC, S], F32R)
        vh, vl = sb("vh", [P, NT, D], F32R), sb("vl", [P, NT, D], F32R)
        vtmp = [sb(f"vtmp{i}", [P, D], F32) for i in range(NT)]
        prob = sb("prob", [P, NT, S], F32)
        ph, pl = y1h, y1l
        y2 = sb("y2", [P, NT, D], F32)
        stats = sb("stats", [P, NT, 6], F32)
        mv = sb("mv", [P, NT, 2], F32)
        veps, rt = sb("veps", [P, NT], F32), sb("rt", [P, NT], F32)
        rstd = [sb(f"rstd{k}", [P, NT], F32) for k in range(3)]
        shift = [sb(f"shift{k}", [P, NT], F32) for k in range(3)]
        krow, smax, mr, nbias, rsum, rinv = (sb(n, [P, NT], F32) for n in ("krow", "smax", "mr", "nbias", "rsum", "rinv"))
        lg = sb("lg", [P, NT, E], F32)
        lmax, lsum, linv = (sb(n, [P, NT], F32) for n in ("lmax", "lsum", "linv"))
        top = sb("top", [P, NT, 8], F32)
        topi = sb("topi", [P, NT, 8], U32)
        eidx = sb("eidx", [P, NT, K], F32)
        oh = sb("oh", [P, K, NT, E], F32)
        picked = sb("picked", [P, NT, E], BF16)
        count = sb("count", [P, E], BF16)
        pos2 = sb("pos2", [P, K, NT, E], F32)
        pos = sb("pos", [P, K, NT], F32)
        slot = sb("slot", [P, K, NT], F32)
        slot_i = sb("slot_i", [P, K, NT], I32)
        hi_i, lo_i = sb("hi_i", [P, K, NT], I32), sb("lo_i", [P, K, NT], I32)
        slot_hi, slot_lo = sb("slot_hi", [P, K, NT], F32), sb("slot_lo", [P, K, NT], F32)
        idw = sb("idw", [P, K, NT], F32)
        gate = sb("gate", [P, K, NT], F32)
        oh_lo = [sb(f"oh_lo{i}", [P, P], F32) for i in range(OS)]
        oh_hi = [sb(f"oh_hi{i}", [P, 2 * NSLOT], F32) for i in range(OS)]

        s_w, s_small = sem("s_w"), sem("s_small")
        s_wraw = [sem(f"s_wraw{i}") for i in range(3)]
        s_x = [sem(f"s_x{i}") for i in range(XS)]
        s_c = sem("s_c")
        s_const, s_pool = sem("s_const"), sem("s_pool")
        s_bkb, s_init, s_wh, s_whi = sem("s_bkb"), sem("s_init"), sem("s_wh"), sem("s_whi")
        s_y0, s_y1, s_y1h = sem("s_y0"), sem("s_y1"), sem("s_y1h")
        s_ch, s_cl = sem("s_ch"), sem("s_cl")
        s_vh, s_vl = sem("s_vh"), sem("s_vl")
        s_qh, s_nb, s_ph = sem("s_qh"), sem("s_nb"), sem("s_ph")
        s_y2, s_base, s_xb = sem("s_y2"), sem("s_base"), sem("s_xb")
        s_stat = [sem(f"s_stat{k}") for k in range(3)]
        s_krow = sem("s_krow")
        s_lg, s_le, s_pick = sem("s_lg"), sem("s_le"), sem("s_pick")
        s_oh, s_ohfree = sem("s_oh"), sem("s_ohfree")
        s_out, s_yout = sem("s_out"), sem("s_yout")
        s_zero, s_pad = sem("s_zero"), sem("s_pad")
        s_dve = sem("s_dve")
        s_count, s_cnt = sem("s_count"), sem("s_cnt")

        order = []
        for i in range(-1, B + 1):
            for name, b in (("Y1T", i), ("V", i), ("Y2T", i - 1), ("LN0", i + 1), ("Q", i), ("G", i + 1),
                            ("INIT", i + 1), ("L", i - 1), ("SC", i), ("T", i + 1), ("X", i - 1), ("PT", i),
                            ("C", i + 1), ("M", i + 1), ("Z", i - 1), ("A", i + 1), ("PV", i)):
                if 0 <= b < (1 if name == "INIT" else B):
                    order.append((name, b))
        block = ctx.enter_context(nc.Block())

        @block.sync
        def _(sp):
            def load_x(b):
                if b >= XS:
                    sp.wait_ge(s_out, 16 * (b - XS + 1))
                sp.dma_start(x[b % XS][:], a["x"][b].rearrange("(t p) d -> p t d", p=P)).then_inc(s_x[b % XS], 16)

            load_x(0)
            sp.dma_start(prob[:], a["WqT"].rearrange("(c p) n -> p c n", p=P)).then_inc(s_wraw[0], 16)
            sp.dma_start(craw[:], a["WkT"].rearrange("(c p) n -> p c n", p=P)).then_inc(s_wraw[1], 16)
            sp.dma_start(y2[:], a["Wv"].rearrange("(c p) n -> p c n", p=P)).then_inc(s_wraw[2], 16)
            for dst, src in ((bias_col[:, 0:NC], a["bq"].rearrange("(c p) -> p c", p=P)),
                             (bias_col[:, NC:2 * NC], a["bk"].rearrange("(c p) -> p c", p=P)),
                             (bv_all[:], a["bv"].partition_broadcast(P)),
                             (rb_all[:], a["rb"].partition_broadcast(P)),
                             (rw[:], a["rw"].rearrange("(c p) e -> p c e", p=P))):
                with nc.allow_non_contiguous_dma(reason="a few columns of biases"):
                    sp.dma_start(dst, src).then_inc(s_small, 16)
            sp.dma_start(CT[:], a["CT"]).then_inc(s_w, 16)
            sp.dma_start(QT[:], a["QT"]).then_inc(s_w, 16)
            load_x(1)
            load_x(2)
            for name, b in order:
                if name == "C":
                    if b == 0:
                        filled(sp, "QB", 0)
                    else:
                        sp.wait_ge(s_cl, NC * b)
                    sp.dma_start(craw[:], a["ctxT"][b].rearrange("(c p) k -> p c k", p=P)).then_inc(s_c, 16)
                if name == "PV":
                    rows = slice(b * S, (b + 1) * S)
                    sp.wait_ge(s_y2, NT * (b + 1))
                    sp.dma_start(Y[rows, :].rearrange("(t p) d -> p t d", p=P), y2[:]).then_inc(s_yout, 16)
                    sp.wait_ge(s_base, NT * (b + 1))
                    sp.dma_start(out[rows, :].rearrange("(t p) d -> p t d", p=P), x[b % XS][:]).then_inc(s_out, 16)
                    if b + XS < B:
                        load_x(b + XS)
            sp.wait_ge(s_yout, 16 * B)
            sp.wait_ge(s_out, 16 * B)

        @block.gpsimd
        def _(pool):
            n_pool = [0]

            def link(ins):
                n_pool[0] += 1
                ins.then_inc(s_pool, 1)
                pool.wait_ge(s_pool, n_pool[0])

            link(pool.memset(ident[:], 0.0))
            pool.affine_select(out=ident[:], in_=ident[:], compare_op=ALU.not_equal, fill=1.0, base=0,
                               pattern=[[-1, P]], channel_multiplier=1).then_inc(s_const, 1)
            link(pool.memset(before[:], 1.0))
            pool.affine_select(out=before[:], in_=before[:], compare_op=ALU.is_gt, fill=0.0, base=0,
                               pattern=[[1, P]], channel_multiplier=-1).then_inc(s_const, 1)
            pool.memset(ones[:], 1.0).then_inc(s_const, 1)
            pool.memset(count[:], 0.0).then_inc(s_const, 1)
            pool.memset(slot_list[:], 0.0).then_inc(s_const, 1)
            pool.memset(magic[:], 0x5F3759E0).then_inc(s_const, 1)
            pool.iota(iota_lo[:], [[1, P]], 0, 0, True).then_inc(s_const, 1)
            pool.iota(iota_e[:], [[1, E]], 0, 0, True).then_inc(s_const, 1)
            pool.iota(token_no[:], [[P, B * NT]], 0, 1, True).then_inc(s_const, 1)
            pool.iota(pad_no[:], [[0, E], [P, ET]], N, 1, True).then_inc(s_const, 1)
            pool.memset(vtmp[0][:], 0.0).then_inc(s_zero, 1)
            pool.wait_ge(s_zero, 1)
            for dst in (Y, out):
                pool.dma_start(dst[N:N + PAD, :].rearrange("(t p) d -> p t d", p=P),
                               vtmp[0][:].unsqueeze(1).to_broadcast([P, PAD // P, D])).then_inc(s_pad, 16)
            pool.wait_ge(s_pad, 32)

            for name, b in order:
                if name == "C":
                    if b >= 1:
                        filled(pool, "SC", b - 1, NT - 1)
                    for c in range(NC):
                        pool.wait_ge(s_ch, NC * b + c + 1)
                        pool.tensor_tensor(cl[:, c, :], craw[:, c, :], ch[:, c, :].bitcast(F32),
                                           ALU.subtract).then_inc(s_cl, 1)
                if name == "V":
                    for t in range(NT):
                        pool.wait_ge(s_vh, NT * b + t + 1)
                        pool.tensor_tensor(vl[:, t, :], vtmp[t][:], vh[:, t, :].bitcast(F32),
                                           ALU.subtract).then_inc(s_vl, 1)
                if name == "PV":
                    for t in range(NT):
                        pool.wait_ge(s_y2, NT * b + t + 1)
                        pool.tensor_tensor(x[b % XS][:, t, :], x[b % XS][:, t, :], y2[:, t, :],
                                           ALU.add).then_inc(s_base, 1)
                if name == "A":
                    for t in range(NT):
                        pool.wait_ge(s_y1, NT * b + t + 1)
                        pool.tensor_tensor(x[b % XS][:, t, :], x[b % XS][:, t, :], bv_all[:], ALU.add)\
                            .then_inc(s_xb, 1)

        @block.scalar
        def _(act):
            def copy(dst, src):
                return act.activation(dst, src, ACT.Copy)

            def normalise(k, dst, b, done):
                act.wait_ge(s_stat[k], b + 1)
                for t in range(NT):
                    act.activation(dst[:, t, :], x[b % XS][:, t, :], ACT.Identity, bias=shift[k][:, t:t + 1],
                                   scale=rstd[k][:, t:t + 1]).then_inc(done, 1)

            def normalise_x2(b):
                if b >= 1:
                    act.wait_ge(s_yout, 16 * b)
                    act.wait_ge(s_base, NT * b)
                    filled(act, "Y2T", b - 1, NC - 1)
                normalise(2, y2, b, s_y2)

            for name, b in order:
                if name == "LN0":
                    if b >= 1:
                        filled(act, "Y1T", b - 1, NC - 1)
                        act.wait_ge(s_krow, b)
                    normalise(0, y, b, s_y0)
                if name == "T":
                    for q in range(H):
                        filled(act, "T", b, q)
                        bank = ps[BANK["T"][q]]
                        copy(y[:, q, :], bank[:]).then_inc(s_ev["T"], 1)
                if name == "M":
                    filled(act, "M", b)
                    bank = ps[BANK["M"][0]]
                    copy(M[:], bank[:]).then_inc(s_ev["M"], 1)
                if name == "A":
                    filled(act, "M", b)
                    normalise(1, y, b, s_y1)
                if name == "PV" and b == B - 1:
                    normalise_x2(b)
                if name == "INIT":
                    act.wait_ge(s_wraw[2], 16)
                    for c in range(NC):
                        copy(VWH[:, c, :], y2[:, c, :]).then_inc(s_wh, 1)
                    for c in range(NC):
                        filled(act, "W", 0, c)
                        bank = ps[BANK["W"][c]]
                        copy(WH[:, c, :], bank[:]).then_inc(s_whi, 1)
                if name == "Y1T":
                    for c in range(NC):
                        filled(act, "Y1T", b, c)
                        bank = ps[BANK["Y1T"][c]]
                        copy(y1h[:, c, :], bank[:]).then_inc(s_y1h, 1)
                if name == "Y2T":
                    act.wait_ge(s_krow, min(b + 2, B))
                    for c in range(NC):
                        filled(act, "Y2T", b, c)
                        bank = ps[BANK["Y2T"][c]]
                        copy(prob[:, c, :], bank[:]).then_inc(s_ev["Y2T"], 1)
                if name == "L":
                    act.wait_ge(s_lg, b + 1)
                    for t in range(NT):
                        act.activation(lg[:, t, :], lg[:, t, :], ACT.Exp, bias=lmax[:, t:t + 1],
                                       accum_out=lsum[:, t:t + 1]).then_inc(s_le, 1)
                if name == "Q":
                    for c in range(NC):
                        filled(act, "Q", b, c)
                        bank = ps[BANK["Q"][c]]
                        act.activation(qh[:, c, :], bank[:], ACT.Identity, bias=qbias[:, 2 * c:2 * c + 1])\
                           .then_inc(s_qh, 1)
                if name == "G":
                    filled(act, "G", b)
                    bank = ps[BANK["G"][0]]
                    copy(G[:], bank[:]).then_inc(s_ev["G"], 1)
                    for c in range(NC):
                        filled(act, "YT", b, c)
                        bank = ps[BANK["YT"][c]]
                        copy(yT[:, c, :], bank[:]).then_inc(s_ev["YT"], 1)
                if name == "SC":
                    for t in range(NT):
                        act.wait_ge(s_nb, NT * b + t + 1)
                        filled(act, "SC", b, t)
                        bank = ps[BANK["SC"][t]]
                        act.activation(prob[:, t, :], bank[:], ACT.Exp, bias=nbias[:, t:t + 1],
                                             scale=SCALE, accum_out=rsum[:, t:t + 1]).then_inc(s_ev["SC"], 1)
                if name == "PT":
                    for c in range(NT):
                        filled(act, "PT", b, c)
                        bank = ps[BANK["PT"][c]]
                        copy(ph[:, c, :], bank[:]).then_inc(s_ph, 1)
                if name == "C":
                    act.wait_ge(s_c, 16 * (b + 1))
                    if b >= 1:
                        filled(act, "SC", b - 1, NT - 1)
                    for c in range(NC):
                        copy(ch[:, c, :], craw[:, c, :]).then_inc(s_ch, 1)
                if name == "V":
                    for t in range(NT):
                        filled(act, "V", b, t)
                        if b >= 1:
                            act.wait_ge(s_vl, NT * (b - 1) + t + 1)
                            filled(act, "PV", b - 1, NT - 1)
                        bank = ps[BANK["V"][t]]
                        copy(vtmp[t][:], bank[:]).then_inc(s_ev["V"], 1)
                        drained(act, "V", b, t)
                        copy(vh[:, t, :], vtmp[t][:]).then_inc(s_vh, 1)
                        if t == 1 and b >= 1:
                            normalise_x2(b - 1)

        @block.vector
        def _(dve):
            n_dve = [0]

            def link(ins):
                n_dve[0] += 1
                ins.then_inc(s_dve, 1)
                dve.wait_ge(s_dve, n_dve[0])

            def inverse_deviation(k):
                link(dve.tensor_scalar(veps[:], mv[:, :, 1], EPS, None, ALU.add))
                link(dve.tensor_scalar(rstd[k][:].bitcast(I32), veps[:].bitcast(I32), 1, -1,
                                       ALU.logical_shift_right, ALU.bitwise_xor))
                link(dve.tensor_tensor(rstd[k][:].bitcast(I32), rstd[k][:].bitcast(I32), magic[:], ALU.add))
                for _ in range(3):
                    link(dve.tensor_tensor(rt[:], rstd[k][:], rstd[k][:], ALU.mult))
                    link(dve.scalar_tensor_tensor(rt[:], rt[:], -0.5, veps[:], ALU.mult, ALU.mult))
                    link(dve.scalar_tensor_tensor(rstd[k][:], rt[:], 1.5, rstd[k][:], ALU.add, ALU.mult))

            def deviations(k, b, used):
                src = x[b % XS]
                for t in range(NT):
                    last = dve.bn_stats(stats[:, t, :], src[:, t, :])
                link(last)
                for t in range(NT):
                    last = dve.bn_aggr(mv[:, t, :], stats[:, t, :])
                link(last)
                dve.wait_ge(used, NT * b)
                inverse_deviation(k)
                dve.scalar_tensor_tensor(shift[k][:], mv[:, :, 0], -1.0, rstd[k][:], ALU.mult, ALU.mult)\
                    .then_inc(s_stat[k], 1)

            dve.wait_ge(s_const, 10)
            for name, b in order:
                if name == "INIT":
                    dve.wait_ge(s_small, 16 * 5)
                    for c in range(NC):
                        last = dve.tensor_copy(M[:, c * P:(c + 1) * P],
                                               bias_col[:, NC + c:NC + c + 1].to_broadcast([P, P]))
                    last.then_inc(s_bkb, 1)
                    for c in range(NC):
                        dve.wait_ge(s_wh, c + 1)
                        last = dve.tensor_tensor(VWL[:, c, :], y2[:, c, :], VWH[:, c, :].bitcast(F32), ALU.subtract)
                    last.then_inc(s_wh, 1)
                    for c in range(NC):
                        dve.wait_ge(s_whi, c + 1)
                        filled(dve, "W", 0, c)
                        bank = ps[BANK["W"][c]]
                        dve.tensor_tensor(WL[:, c, :], bank[:], WH[:, c, :].bitcast(F32), ALU.subtract).then_inc(s_ev["W"], 1)
                    filled(dve, "KR", 0)
                    bank = ps[BANK["KR"][0]]
                    dve.tensor_copy(key_row[:], bank[:]).then_inc(s_ev["KR"], 1)
                    filled(dve, "QB", 0)
                    bank = ps[BANK["QB"][0]]
                    dve.tensor_copy(qbias[:], bank[:, 0:2 * NC + 1]).then_inc(s_ev["QB"], 1)
                    drained(dve, "QB", 0)
                if name == "LN0":
                    dve.wait_ge(s_x[b % XS], 16 * (b // XS + 1))
                    deviations(0, b, s_y0)
                if name == "A":
                    for t in range(NT):
                        filled(dve, "A", b, t)
                        bank = ps[BANK["A"][t]]
                        dve.tensor_tensor(x[b % XS][:, t, :], bank[:], x[b % XS][:, t, :], ALU.add).then_inc(s_ev["A"], 1)
                    drained(dve, "A", b, NT - 1)
                    deviations(1, b, s_y1)
                if name == "Y1T":
                    dve.wait_ge(s_y1, NT * (b + 1))
                    if b >= 1:
                        filled(dve, "PT", b - 1, NT - 1)
                    for t in range(NT):
                        last = dve.tensor_tensor_reduce(prob[:, t, :], y[:, t, :], key_row[:], 1.0, 0.0,
                                                        ALU.mult, ALU.add, krow[:, t:t + 1])
                    link(last)
                    dve.tensor_scalar(krow[:], krow[:], qbias[:, 2 * NC:2 * NC + 1], None, ALU.add)\
                        .then_inc(s_krow, 1)
                    for c in range(NC):
                        dve.wait_ge(s_y1h, NC * b + c + 1)
                        filled(dve, "Y1T", b, c)
                        bank = ps[BANK["Y1T"][c]]
                        dve.tensor_tensor(y1l[:, c, :], bank[:], y1h[:, c, :].bitcast(F32), ALU.subtract).then_inc(s_ev["Y1T"], 1)
                if name == "Q":
                    for c in range(NC):
                        dve.wait_ge(s_qh, NC * b + c + 1)
                        filled(dve, "Q", b, c)
                        bank = ps[BANK["Q"][c]]
                        dve.scalar_tensor_tensor(ql[:, c, :], bank[:], qbias[:, 2 * c:2 * c + 1],
                                                       qh[:, c, :].bitcast(F32), ALU.add, ALU.subtract).then_inc(s_ev["Q"], 1)
                if name == "SC":
                    dve.wait_ge(s_krow, b + 1)
                    for t in range(NT):
                        filled(dve, "SC", b, t)
                        bank = ps[BANK["SC"][t]]
                        link(dve.reduce_max(smax[:, t:t + 1], bank[:], AX_X))
                        link(dve.tensor_tensor(mr[:, t:t + 1], smax[:, t:t + 1], krow[:, t:t + 1], ALU.add))
                        dve.tensor_scalar(nbias[:, t:t + 1], mr[:, t:t + 1], krow[:, t:t + 1], -SCALE,
                                          ALU.subtract, ALU.mult).then_inc(s_nb, 1)
                if name == "PT":
                    for c in range(NT):
                        dve.wait_ge(s_ph, NT * b + c + 1)
                        filled(dve, "PT", b, c)
                        bank = ps[BANK["PT"][c]]
                        dve.tensor_tensor(pl[:, c, :], bank[:], ph[:, c, :].bitcast(F32), ALU.subtract).then_inc(s_ev["PT"], 1)
                if name == "PV":
                    drained(dve, "SC", b, NT - 1)
                    link(dve.reciprocal(rinv[:], rsum[:]))
                    for t in range(NT):
                        filled(dve, "PV", b, t)
                        dve.wait_ge(s_xb, NT * b + t + 1)
                        bank = ps[BANK["PV"][t]]
                        dve.scalar_tensor_tensor(x[b % XS][:, t, :], bank[:], rinv[:, t:t + 1],
                                                       x[b % XS][:, t, :], ALU.mult, ALU.add).then_inc(s_ev["PV"], 1)
                    drained(dve, "PV", b, NT - 1)
                    deviations(2, b, s_y2)
                if name == "L":
                    filled(dve, "L", b)
                    bank = ps[BANK["L"][0]]
                    dve.tensor_tensor(lg[:], bank[:, 0:NT * E].rearrange("p (t e) -> p t e", e=E),
                                            rb_all[:].unsqueeze(1).to_broadcast([P, NT, E]), ALU.add).then_inc(s_ev["L"], 1)
                    drained(dve, "L", b)
                    dve.tensor_reduce(lmax[:], lg[:], AX_X, ALU.max, negate=True).then_inc(s_lg, 1)
                    dve.wait_ge(s_le, NT * (b + 1))
                    link(dve.reciprocal(linv[:], lsum[:]))
                    link(dve.tensor_tensor(lg[:], lg[:], linv[:].unsqueeze(2).to_broadcast([P, NT, E]), ALU.mult))
                    for t in range(NT):
                        last = dve.max(top[:, t, :], lg[:, t, :])
                    link(last)
                    for t in range(NT):
                        last = dve.max_index(topi[:, t, :], top[:, t, :], lg[:, t, :])
                    link(last)
                    link(dve.tensor_copy(eidx[:], topi[:, :, 0:K]))
                    for k in range(K):
                        last = dve.tensor_tensor(oh[:, k], iota_e[:].unsqueeze(1).to_broadcast([P, NT, E]),
                                                 eidx[:, :, k:k + 1].to_broadcast([P, NT, E]), ALU.is_equal)
                    link(last)
                    dve.tensor_tensor(picked[:], oh[:, 0], oh[:, 1], ALU.add).then_inc(s_pick, 1)
                    link(dve.tensor_tensor(linv[:], top[:, :, 0], top[:, :, 1], ALU.add))
                    link(dve.tensor_scalar(linv[:], linv[:], 1e-9, None, ALU.add))
                    link(dve.reciprocal(linv[:], linv[:]))
                    for k in range(K):
                        dve.tensor_tensor(gate[:, k, :], top[:, :, k], linv[:], ALU.mult).then_inc(s_count, 1)
                if name == "X":
                    filled(dve, "X", b)
                    bank = ps[BANK["X"][0]]
                    for k in range(K):
                        last = dve.tensor_tensor(pos2[:, k], bank[:, 0:NT * E].rearrange("p (t e) -> p t e", e=E),
                                                 oh[:, k], ALU.mult)
                    last.then_inc(s_ev["X"], 1)
                    drained(dve, "X", b)
                    link(dve.tensor_reduce(pos[:], pos2[:], AX_X, ALU.add))
                    link(dve.tensor_scalar(slot[:], pos[:], float(CAP), float(1 << 16), ALU.is_ge, ALU.mult))
                    link(dve.tensor_tensor(slot[:], slot[:], pos[:], ALU.add))
                    for k in range(K):
                        last = dve.scalar_tensor_tensor(slot[:, k], eidx[:, :, k], float(CAP), slot[:, k],
                                                        ALU.mult, ALU.add)
                    link(last)
                    link(dve.tensor_copy(slot_i[:], slot[:]))
                    dve.tensor_scalar(lo_i[:], slot_i[:], P - 1, None, ALU.bitwise_and)
                    link(dve.tensor_scalar(hi_i[:], slot_i[:], 7, None, ALU.logical_shift_right))
                    dve.tensor_copy(slot_lo[:], lo_i[:]).then_inc(s_count, 1)
                    dve.tensor_copy(slot_hi[:], hi_i[:]).then_inc(s_count, 1)
                    for k in range(K):
                        last = dve.scalar_tensor_tensor(idw[:, k], pos[:, k], -1.0,
                                                        token_no[:, b * NT:(b + 1) * NT], ALU.mult, ALU.add)
                    link(last)
                    dve.tensor_scalar(idw[:], idw[:], -float(N), None, ALU.add).then_inc(s_count, 1)
                    for t in range(NT):
                        last = dve.tensor_tensor(count[:], count[:], picked[:, t, :], ALU.add)
                        if t < NT - 1:
                            link(last)
                    last.then_inc(s_cnt, 1)
                    dve.wait_ge(s_cnt, b + 1)
                if name == "Z":
                    dve.wait_ge(s_count, 5 * (b + 1))
                    for n in range(K * NT):
                        k, t = divmod(n, NT)
                        if n >= OS:
                            dve.wait_ge(s_ohfree, (K * NT - 1) * b + n - OS + 1)
                        hi = slot_hi[:, k, t:t + 1]
                        dve.tensor_scalar(oh_lo[n % OS][:], iota_lo[:], slot_lo[:, k, t:t + 1], None,
                                          ALU.is_equal).then_inc(s_oh, 1)
                        dve.tensor_scalar(oh_hi[n % OS][:, 0:NSLOT], iota_lo[:, 0:NSLOT], hi,
                                          idw[:, k, t:t + 1], ALU.is_equal, ALU.mult).then_inc(s_oh, 1)
                        dve.tensor_scalar(oh_hi[n % OS][:, NSLOT:2 * NSLOT], iota_lo[:, 0:NSLOT], hi,
                                          gate[:, k, t:t + 1], ALU.is_equal, ALU.mult).then_inc(s_oh, 1)
                    filled(dve, "Z", b)
                    bank = ps[BANK["Z"][0]]
                    dve.tensor_tensor(slot_list[:], bank[:, 0:2 * NSLOT], slot_list[:], ALU.add).then_inc(s_ev["Z"], 1)
                    drained(dve, "Z", b)
            dve.tensor_tensor(slot_index[:], slot_list[:, 0:NSLOT], pad_no[:], ALU.add).then_inc(s_dve, 1)

        @block.tensor
        def _(pe):
            def f32_group(out, pairs):
                for i, (left, right) in enumerate(pairs):
                    last = pe.matmul(out, left, right, start=(i == 0), stop=(i == len(pairs) - 1))
                return last

            def transposes(step, src, c):
                for t in range(NT):
                    last = pe.transpose(ps[BANK[step][c]][:, t * P:(t + 1) * P], src[:, t, c * P:(c + 1) * P],
                                        ident[:])
                last.then_inc(s_mm[step], 1)

            pe.wait_ge(s_const, 10)
            for name, b in order:
                if name == "INIT":
                    drained(pe, "G", 0)
                    drained(pe, "YT", 0, NC - 1)
                    pe.wait_ge(s_wraw[0], 16)
                    pe.wait_ge(s_wraw[1], 16)
                    for c in range(NC):
                        f32_group(ps[BANK["W"][c]][:], [(prob[:, j, c * P:(c + 1) * P], craw[:, j, :])
                                                        for j in range(NC)]).then_inc(s_mm["W"], 1)
                    pe.wait_ge(s_bkb, 1)
                    pe.wait_ge(s_small, 16 * 5)
                    f32_group(ps[BANK["KR"][0]][:], [(M[:, j * P:(j + 1) * P], prob[:, j, :])
                                                     for j in range(NC)]).then_inc(s_mm["KR"], 1)
                    bank = ps[BANK["QB"][0]]
                    for c in range(NC):
                        f32_group(bank[:, 2 * c:2 * c + 2],
                                  [(craw[:, j, c * P:(c + 1) * P], bias_col[:, j:j + 2]) for j in range(NC)])
                    f32_group(bank[:, 2 * NC:2 * NC + 1], [(M[:, j * P:(j + 1) * P], bias_col[:, j:j + 1])
                                                           for j in range(NC)]).then_inc(s_mm["QB"], 1)
                if name == "V":
                    if b == 0:
                        pe.wait_ge(s_wh, NC + 1)
                    pe.wait_ge(s_cl, NC * (b + 1))
                    drained(pe, "PV", b - 1, 3)
                    drained(pe, "A", b, 2)
                    for t in range(NT):
                        cols = slice(t * P, (t + 1) * P)
                        three_pass(pe, ps[BANK["V"][t]][:], [(ch[:, c, cols], cl[:, c, cols], VWH[:, c, :], VWL[:, c, :])
                                                             for c in range(NC)]).then_inc(s_mm["V"], 1)
                if name == "Y1T":
                    pe.wait_ge(s_y1, NT * (b + 1))
                    drained(pe, "PV", b - 1, 2)
                    for c in range(NC):
                        transposes("Y1T", y, c)
                if name == "Y2T":
                    pe.wait_ge(s_y2, NT * (b + 1))
                    for c in range(NC):
                        drained(pe, "Y1T", b + 1, c)
                        transposes("Y2T", y2, c)
                if name == "L":
                    drained(pe, "Y2T", b, NC - 1)
                    drained(pe, "Q", b + 1, 1)
                    for t in range(NT):
                        last = f32_group(ps[BANK["L"][0]][:, t * E:(t + 1) * E],
                                         [(prob[:, c, t * P:(t + 1) * P], rw[:, c, :]) for c in range(NC)])
                    last.then_inc(s_mm["L"], 1)
                if name == "Q":
                    drained(pe, "Y1T", b, NC - 1)
                    if b == 0:
                        drained(pe, "W", 0, NC - 1)
                        drained(pe, "QB", 0)
                    for c in range(NC):
                        drained(pe, "V", b, c)
                        cols = slice(c * P, (c + 1) * P)
                        three_pass(pe, ps[BANK["Q"][c]][:], [(WH[:, j, cols], WL[:, j, cols], y1h[:, j, :], y1l[:, j, :])
                                                             for j in range(NC)]).then_inc(s_mm["Q"], 1)
                if name == "X":
                    pe.wait_ge(s_pick, b + 1)
                    drained(pe, "SC", b + 1, 0)
                    pe.wait_ge(s_cnt, b)
                    for t in range(NT):
                        pairs = [(before[:], picked[:, t, :])] + [(ones[:], picked[:, i, :]) for i in range(t)]
                        last = f32_group(ps[BANK["X"][0]][:, t * E:(t + 1) * E], pairs + [(ones[:], count[:])])
                    last.then_inc(s_mm["X"], 1)
                if name == "G":
                    pe.wait_ge(s_y0, NT * (b + 1))
                    drained(pe, "Y2T", b - 2, 3)
                    for q in range(H):
                        cols = slice(q * P, (q + 1) * P)
                        last = f32_group(ps[BANK["G"][0]][:, cols], [(y[:, t, cols], y[:, t, cols]) for t in range(NT)])
                    last.then_inc(s_mm["G"], 1)
                    drained(pe, "Q", b - 1, 0)
                    for c in range(NC):
                        transposes("YT", y, c)
                if name == "SC":
                    drained(pe, "Q", b, NC - 1)
                    drained(pe, "G", b + 1)
                    drained(pe, "YT", b + 1, 0)
                    for t in range(NT):
                        cols = slice(t * P, (t + 1) * P)
                        three_pass(pe, ps[BANK["SC"][t]][:], [(qh[:, c, cols], ql[:, c, cols], ch[:, c, :], cl[:, c, :])
                                                              for c in range(NC)]).then_inc(s_mm["SC"], 1)
                if name == "Z":
                    drained(pe, "T", b + 2, 2)
                    for n in range(K * NT):
                        m = K * NT * b + n
                        pe.wait_ge(s_oh, 3 * (m + 1))
                        last = pe.matmul(ps[BANK["Z"][0]][:, 0:2 * NSLOT], oh_lo[n % OS][:], oh_hi[n % OS][:],
                                         start=(n == 0), stop=(n == K * NT - 1))
                        last.then_inc(s_ohfree if n < K * NT - 1 else s_mm["Z"], 1)
                if name == "T":
                    if b == 0:
                        pe.wait_ge(s_w, 32)
                    drained(pe, "G", b)
                    drained(pe, "YT", b, 3)
                    drained(pe, "L", b - 2)
                    if b == 0:
                        drained(pe, "W", 0, NC - 1)
                        drained(pe, "QB", 0)
                    for q in range(H):
                        pe.matmul(ps[BANK["T"][q]][:], G[:, q * P:(q + 1) * P], CT[:, q, :],
                                  start=True, stop=True).then_inc(s_mm["T"], 1)
                if name == "PT":
                    drained(pe, "SC", b, NT - 1)
                    drained(pe, "T", b + 1, 0)
                    for c in range(NT):
                        transposes("PT", prob, c)
                if name == "M":
                    drained(pe, "T", b, H - 1)
                    for h in range(H):
                        cols = slice(h * P, (h + 1) * P)
                        last = f32_group(ps[BANK["M"][0]][:, cols], [(QT[:, h, q, :], y[:, q, cols]) for q in range(H)])
                    last.then_inc(s_mm["M"], 1)
                if name == "PV":
                    drained(pe, "PT", b, NT - 1)
                    pe.wait_ge(s_vl, NT * (b + 1))
                    drained(pe, "M", b + 1)
                    drained(pe, "Z", b - 1)
                    for t in range(NT):
                        cols = slice(t * P, (t + 1) * P)
                        three_pass(pe, ps[BANK["PV"][t]][:], [(ph[:, c, cols], pl[:, c, cols], vh[:, c, :], vl[:, c, :])
                                                              for c in range(NT)]).then_inc(s_mm["PV"], 1)
                if name == "A":
                    drained(pe, "M", b)
                    drained(pe, "YT", b, NC - 1)
                    drained(pe, "X", b - 2)
                    drained(pe, "PT", b - 1, 1)
                    for t in range(NT):
                        for h in range(H):
                            cols = slice(h * P, (h + 1) * P)
                            last = pe.matmul(ps[BANK["A"][t]][:, cols], yT[:, h, t * P:(t + 1) * P], M[:, cols],
                                             start=True, stop=True)
                        last.then_inc(s_mm["A"], 1)


def phase2(nc, a, Y, shared):
    out = a["out"]
    ident, slot_list, slot_index = shared["ident"], shared["slot_list"], shared["slot_index"]
    RING = 22
    RAW = 6
    TMP = 3
    with ExitStack() as ctx:
        def sb(name, shape, dt):
            return ctx.enter_context(nc.sbuf_tensor(name, shape, dt))

        def sem(name):
            return ctx.enter_context(nc.semaphore(name))

        ps = [ctx.enter_context(nc.psum_tensor(f"ps_m{i}", [P, 512], F32)) for i in range(BANKS)]
        gate_bank = [ps[0], ps[2]]
        up_bank = [ps[1], ps[3]]
        down_bank = [ps[4], ps[5]]
        x_bank = [ps[6], ps[7]]
        wraw = [sb(f"wraw{i}", [P, D], F32) for i in range(RAW)]
        wh = [sb(f"wh{i}", [P, D], F32R) for i in range(RING)]
        wl = [sb(f"wl{i}", [P, D], F32R) for i in range(RING)]
        xn = [sb(f"xn{i}", [P, ET, D], F32) for i in range(2)]
        xh, xl = sb("xh", [P, NC, CAP], F32R), sb("xl", [P, NC, CAP], F32R)
        hh, hl = sb("hh", [P, FC, CAP], F32R), sb("hl", [P, FC, CAP], F32R)
        silu = [sb(f"silu{i}", [P, 512], F32) for i in range(TMP)]
        ht = [sb(f"ht{i}", [P, 512], F32) for i in range(TMP)]
        ost = sb("ost", [P, ET, D], F32)

        s_zero, s_raw = sem("t_zero"), [sem(f"t_raw{i}") for i in range(RAW)]
        s_wh, s_wl = sem("t_wh"), sem("t_wl")
        s_xn = [sem("t_xn0"), sem("t_xn1")]
        s_xg = [sem("t_xg0"), sem("t_xg1")]
        s_xT, s_xh, s_xl = sem("t_xT"), sem("t_xh"), sem("t_xl")
        s_gu, s_silu, s_ht, s_hh, s_hl = sem("t_gu"), sem("t_silu"), sem("t_ht"), sem("t_hh"), sem("t_hl")
        s_down, s_ost = sem("t_down"), sem("t_ost")
        s_add = [sem(f"t_add{i}") for i in range(ET)]

        groups = [(0, g, NT, g == B - 1) for g in range(B)] + [(1 + e, e, ET, True) for e in range(E)]
        NG = len(groups)
        tiles_of = [tiles for _, _, tiles, _ in groups]
        tiles_before = [sum(tiles_of[:g]) for g in range(NG + 1)]

        def cuts(g):
            n = tiles_of[g] * P
            return [(0, n)] if n <= 512 else [(0, n // 2), (n // 2, n // 2)]

        units = [(g, c, j) for g in range(NG) for c in range(FC) for j in range(len(cuts(g)))]
        unit_no = {u: n for n, u in enumerate(units)}
        n_chunks = (1 + E) * WC
        FIRST = 4
        EACH = -(-(RING - FIRST) // FC)

        def split_after(g, step):
            job, _, _, last = groups[g]
            if g == 0 and step != "down":
                return list(range(FIRST + step * EACH, min(FIRST + (step + 1) * EACH, RING)))
            if not last:
                return []
            done = range(GU, WC) if step == "down" else range(2 * step, min(2 * step + 2, GU))
            return [job * WC + i + RING for i in done if job * WC + i + RING < n_chunks]

        def wait_last_use(eng, n):
            job, i = divmod(n, WC)
            g = B - 1 + job
            if i < GU:
                eng.wait_ge(s_gu, unit_no[(g, i // 2, len(cuts(g)) - 1)] + 1)
            else:
                eng.wait_ge(s_down, tiles_before[g + 1])

        def adds_of(g, t):
            return sum(tiles > t for tiles in tiles_of[:g])

        def rows_of(c):
            return P if c < FC - 1 else FH

        def tail(g):
            after = tiles_of[g + 1] if g + 1 < NG else 0
            for t in range(max(tiles_of[g], after)):
                if t < after:
                    yield "x", g + 1, t
                if t < tiles_of[g]:
                    yield "down", g, t

        block = ctx.enter_context(nc.Block())

        @block.sync
        def _(sp):
            def load_tokens(g):
                if g >= 2:
                    sp.wait_ge(s_xT, tiles_before[g - 1])
                sp.dma_start(xn[g % 2][:, 0:NT, :], Y[g * S:(g + 1) * S, :].rearrange("(t p) d -> p t d", p=P))\
                  .then_inc(s_xn[g % 2], 16)

            load_tokens(0)
            for n in range(n_chunks):
                if n >= RAW:
                    sp.wait_ge(s_wl, n - RAW + 1)
                job, i = divmod(n, WC)
                sp.dma_start(wraw[n % RAW][:], a["wts"][job, :, i * D:(i + 1) * D]).then_inc(s_raw[n % RAW], 16)
                if n == RING - 1:
                    for g in range(1, B):
                        load_tokens(g)

        @block.gpsimd
        def _(pool):
            def split(n):
                pool.wait_ge(s_wh, n + 1)
                pool.tensor_tensor(wl[n % RING][:], wraw[n % RAW][:], wh[n % RING][:].bitcast(F32),
                                   ALU.subtract).then_inc(s_wl, 1)

            def slots(e, t):
                return bass.IndirectOffsetOnAxis(ap=slot_index[:, e * ET + t:e * ET + t + 1], axis=0)

            def gather(g):
                pool.wait_ge(s_xT, tiles_before[g - 1])
                for t in range(ET):
                    pool.indirect_dma_start(xn[g % 2][:, t, :], None, Y[:, :], slots(groups[g][1], t),
                                            bounds_check=N + PAD - 1).then_inc(s_xg[g % 2], 16)

            for n in range(FIRST):
                split(n)
            for g, (job, part, tiles, last) in enumerate(groups):
                if g + 1 < NG and groups[g + 1][0] > 0:
                    gather(g + 1)
                for c in range(FC):
                    for n in split_after(g, c):
                        split(n)
                for t in range(tiles):
                    pool.wait_ge(s_ost, tiles_before[g] + t + 1)
                    if job == 0:
                        pool.dma_start(out[part * S + t * P:part * S + (t + 1) * P, :], ost[:, t, :],
                                       accum_op=ALU.add).then_inc(s_add[t], 16)
                        continue
                    if t == 0:
                        for i in range(ET):
                            pool.wait_ge(s_add[i], 16 * adds_of(g, i))
                    pool.indirect_dma_start(out[:, :], slots(part, t), ost[:, t, :], None,
                                            bounds_check=N + PAD - 1, compute_op=ALU.add).then_inc(s_add[t], 16)
                for n in split_after(g, "down"):
                    split(n)
            for i in range(ET):
                pool.wait_ge(s_add[i], 16 * adds_of(NG, i))

        @block.scalar
        def _(act):
            def copy(dst, src):
                return act.activation(dst, src, ACT.Copy)

            def split(n):
                act.wait_ge(s_raw[n % RAW], 16 * (n // RAW + 1))
                if n >= RING:
                    wait_last_use(act, n - RING)
                copy(wh[n % RING][:], wraw[n % RAW][:]).then_inc(s_wh, 1)

            def x_hi(g, t):
                n = tiles_before[g] + t
                act.wait_ge(s_xT, n + 1)
                copy(xh[:, :, t * P:(t + 1) * P], x_bank[n % 2][:].rearrange("p (c n) -> p c n", c=NC))\
                    .then_inc(s_xh, 1)

            def h_hi(u):
                g, c, j = units[u]
                first, n = cuts(g)[j]
                act.wait_ge(s_ht, u + 1)
                copy(hh[0:rows_of(c), c, first:first + n], ht[u % TMP][0:rows_of(c), 0:n]).then_inc(s_hh, 1)

            for t in range(NT):
                x_hi(0, t)
            for n in range(FIRST):
                split(n)
            for g in range(NG):
                for c in range(FC):
                    for j, (first, n) in enumerate(cuts(g)):
                        u = unit_no[(g, c, j)]
                        if u >= TMP:
                            act.wait_ge(s_ht, u - TMP + 1)
                        act.wait_ge(s_gu, u + 1)
                        bank = gate_bank[u % 2] if c < FC - 1 else up_bank[u % 2]
                        act.activation(silu[u % TMP][0:rows_of(c), 0:n], bank[0:rows_of(c), 0:n], ACT.Silu)\
                           .then_inc(s_silu, 1)
                        if u > unit_no[(g, 0, 0)]:
                            h_hi(u - 1)
                    if c > 0:
                        for m in split_after(g, c - 1):
                            split(m)
                h_hi(u)
                for m in split_after(g, FC - 1):
                    split(m)
                for what, gx, t in tail(g):
                    if what == "x":
                        x_hi(gx, t)
                for m in split_after(g, "down"):
                    split(m)

        @block.vector
        def _(dve):
            def x_lo(g, t):
                n = tiles_before[g] + t
                dve.wait_ge(s_xh, n + 1)
                cols = slice(t * P, (t + 1) * P)
                dve.tensor_tensor(xl[:, :, cols], x_bank[n % 2][:].rearrange("p (c n) -> p c n", c=NC),
                                  xh[:, :, cols].bitcast(F32), ALU.subtract).then_inc(s_xl, 1)

            def h_lo(u):
                g, c, j = units[u]
                first, n = cuts(g)[j]
                rows = rows_of(c)
                dve.wait_ge(s_hh, u + 1)
                dve.tensor_tensor(hl[0:rows, c, first:first + n], ht[u % TMP][0:rows, 0:n],
                                  hh[0:rows, c, first:first + n].bitcast(F32), ALU.subtract).then_inc(s_hl, 1)

            dve.memset(hh[FH:P, FC - 1, :].bitcast(F32), 0.0).then_inc(s_zero, 1)
            dve.memset(hl[FH:P, FC - 1, :].bitcast(F32), 0.0).then_inc(s_zero, 1)
            for t in range(NT):
                x_lo(0, t)
            for g, (job, part, _, _) in enumerate(groups):
                for c in range(FC):
                    for j, (first, n) in enumerate(cuts(g)):
                        u = unit_no[(g, c, j)]
                        if u >= TMP:
                            dve.wait_ge(s_hl, u - TMP + 1)
                        dve.wait_ge(s_silu, u + 1)
                        rows = slice(0, P) if c < FC - 1 else slice(FH, 2 * FH)
                        dve.tensor_tensor(ht[u % TMP][0:rows_of(c), 0:n], up_bank[u % 2][rows, 0:n],
                                          silu[u % TMP][0:rows_of(c), 0:n], ALU.mult).then_inc(s_ht, 1)
                        if u > unit_no[(g, 0, 0)]:
                            h_lo(u - 1)
                h_lo(u)
                for what, gx, t in tail(g):
                    if what == "x":
                        x_lo(gx, t)
                        continue
                    n = tiles_before[g] + t
                    dve.wait_ge(s_down, n + 1)
                    if adds_of(g, t):
                        dve.wait_ge(s_add[t], 16 * adds_of(g, t))
                    if job == 0:
                        dve.tensor_copy(ost[:, t, :], down_bank[n % 2][:]).then_inc(s_ost, 1)
                    else:
                        gate = NSLOT + part * ET + t
                        dve.tensor_scalar(ost[:, t, :], down_bank[n % 2][:], slot_list[:, gate:gate + 1], None,
                                          ALU.mult).then_inc(s_ost, 1)

        @block.tensor
        def _(pe):
            def transpose_tile(g, t):
                n = tiles_before[g] + t
                if t == 0 and groups[g][0] == 0:
                    pe.wait_ge(s_xn[g % 2], 16 * (g // 2 + 1))
                if groups[g][0] > 0:
                    pe.wait_ge(s_xg[g % 2], 16 * ET * ((g - B) // 2 + 1))
                if n >= 2:
                    pe.wait_ge(s_xl, n - 1)
                for c in range(NC):
                    ins = pe.transpose(x_bank[n % 2][:, c * P:(c + 1) * P], xn[g % 2][:, t, c * P:(c + 1) * P],
                                       ident[:])
                ins.then_inc(s_xT, 1)

            pe.wait_ge(s_zero, 2)
            for t in range(NT):
                transpose_tile(0, t)
            for g, (job, _, tiles, _) in enumerate(groups):
                base = job * WC
                pe.wait_ge(s_xl, tiles_before[g + 1])
                for c in range(FC):
                    for j, (first, n) in enumerate(cuts(g)):
                        u = unit_no[(g, c, j)]
                        if u >= 2:
                            pe.wait_ge(s_ht, u - 1)
                        cols = slice(first, first + n)
                        chunks = ([(gate_bank, 2 * c)] if c < FC - 1 else []) + [(up_bank, min(2 * c + 1, GU - 1))]
                        for bank, i in chunks:
                            m = base + i
                            pe.wait_ge(s_wl, m + 1)
                            ins = three_pass(pe, bank[u % 2][:, 0:n], [
                                (wh[m % RING][:, d * P:(d + 1) * P], wl[m % RING][:, d * P:(d + 1) * P],
                                 xh[:, d, cols], xl[:, d, cols]) for d in range(NC)])
                        ins.then_inc(s_gu, 1)
                for what, gx, t in tail(g):
                    if what == "x":
                        transpose_tile(gx, t)
                        continue
                    n = tiles_before[g] + t
                    if n >= 2:
                        pe.wait_ge(s_ost, n - 1)
                    cols = slice(t * P, (t + 1) * P)
                    for c in range(FC):
                        m = base + GU + c
                        if t == 0:
                            pe.wait_ge(s_wl, m + 1)
                            pe.wait_ge(s_hl, unit_no[(g, c, len(cuts(g)) - 1)] + 1)
                        for i, (left, right) in enumerate(((hh, wh), (hh, wl), (hl, wh))):
                            ins = pe.matmul(down_bank[n % 2][:], left[:, c, cols], right[m % RING][:],
                                            start=(c == 0 and i == 0), stop=(c == FC - 1 and i == 2))
                    ins.then_inc(s_down, 1)


def kernel(x, ctx_1024, L0_attn_queries, L0_attn_combiners, L0_xattn_Wq, L0_xattn_bq, L0_xattn_Wk, L0_xattn_bk,
           L0_xattn_Wv, L0_xattn_bv, L0_ffn_router_w, L0_ffn_router_b, L0_ffn_w_gate, L0_ffn_w_up, L0_ffn_w_down,
           L0_ffn_sw_gate, L0_ffn_sw_up, L0_ffn_sw_down):
    import numpy as np
    import concourse.bacc as bacc
    from concourse.bass_utils import run_bass_kernel_spmd

    def chunks(gate, up, down):
        j = gate.shape[0]
        full = (FC - 1) * P
        g = gate.reshape(j, NC, P, F)
        u = up.reshape(j, NC, P, F)
        pairs = np.stack([g[..., :full].reshape(j, NC, P, FC - 1, P), u[..., :full].reshape(j, NC, P, FC - 1, P)], 4)
        pairs = pairs.transpose(0, 2, 3, 4, 1, 5).reshape(j, P, (GU - 1) * D)
        mixed = np.concatenate([g[..., full:], u[..., full:]], 3).transpose(0, 2, 1, 3).reshape(j, P, D)
        d = np.pad(down, ((0, 0), (0, FC * P - F), (0, 0))).reshape(j, FC, P, D).transpose(0, 2, 1, 3)
        return np.concatenate([pairs, mixed, d.reshape(j, P, FC * D)], 2)

    q = np.asarray(L0_attn_queries).reshape(H, P, H, P)
    c = np.asarray(L0_attn_combiners).reshape(H, H, P, P)
    gate, up, down, sgate, sup, sdown = (np.asarray(w) for w in (
        L0_ffn_w_gate, L0_ffn_w_up, L0_ffn_w_down, L0_ffn_sw_gate, L0_ffn_sw_up, L0_ffn_sw_down))
    arrays = {
        "x": np.asarray(x),
        "ctxT": np.ascontiguousarray(np.asarray(ctx_1024).transpose(0, 2, 1)),
        "QT": np.ascontiguousarray(q.transpose(3, 0, 2, 1)),
        "CT": np.ascontiguousarray(c.transpose(2, 1, 0, 3)).reshape(P, H, H * P),
        "WqT": np.ascontiguousarray(np.asarray(L0_xattn_Wq).T),
        "WkT": np.ascontiguousarray(np.asarray(L0_xattn_Wk).T),
        "Wv": np.asarray(L0_xattn_Wv),
        "bq": np.asarray(L0_xattn_bq), "bk": np.asarray(L0_xattn_bk), "bv": np.asarray(L0_xattn_bv),
        "rw": np.asarray(L0_ffn_router_w), "rb": np.asarray(L0_ffn_router_b),
        "wts": np.concatenate([chunks(sgate[None], sup[None], sdown[None]), chunks(gate, up, down)], 0),
    }
    nc = bacc.Bacc("TRN2", target_bir_lowering=False, num_devices=1)
    args = {k: nc.dram_tensor(f"in_{k}", v.shape, F32, kind="ExternalInput").ap() for k, v in arrays.items()}
    args["out"] = nc.dram_tensor("out_tokens", (N + PAD, D), F32, kind="ExternalOutput").ap()
    build(nc, args)
    r = run_bass_kernel_spmd(nc, [{f"in_{k}": v for k, v in arrays.items()}], core_ids=[0])
    return r.results[0]["out_tokens"][:N].reshape(B, S, D)
```

```python
from contextlib import ExitStack

import concourse.bass as bass
from concourse import mybir

F32 = mybir.dt.float32
F32R = mybir.dt.float32r
BF16 = mybir.dt.bfloat16
I32 = mybir.dt.int32
U32 = mybir.dt.uint32
ALU = mybir.AluOpType
ACT = mybir.ActivationFunctionType
AX_X = mybir.AxisListType.X

P = 128
B, S, D = 8, 512, 512
NT = S // P
NC = D // P
H = NC
N = B * S
E, K, F = 16, 2, 704
CAP = -(-5 * N * K // (4 * E))
ET = CAP // P
NSLOT = E * ET
FC = -(-F // P)
FH = F - (FC - 1) * P
GU = 2 * (FC - 1) + 1
WC = GU + FC
PAD = CAP
EPS = 1e-5
SCALE = float(D) ** -0.5
BANKS = 8
ROWS = 98
XS = 3


def three_pass(pe, out, parts, between=()):
    last = None
    todo = []
    for lh, ll, rh, rl in parts:
        todo += [(lh, rh), (lh, rl), (ll, rh)]
    for i, (left, right) in enumerate(todo):
        last = pe.matmul(out, left, right, start=(i == 0), stop=(i == len(todo) - 1))
        if i % 3 == 2 and between:
            between.pop(0)()
    return last


def build(nc, a):
    Y = nc.dram_tensor("tokens_normed", (N + PAD, D), F32, kind="Internal").ap()
    with ExitStack() as ctx:
        def sb(name, shape, dt):
            return ctx.enter_context(nc.sbuf_tensor(name, shape, dt))

        base, _ = nc.bump_sbuf(ROWS * D * 4)
        placed = []

        def at(row, shape, dt=F32):
            placed.append(row)
            return nc.alloc_sbuf_tensor_at(f"buffer{len(placed)}", [P] + shape, dt, offset=base + int(row * D * 4))

        shared = {
            "ident": sb("ident", [P, P], F32),
            "slot_list": sb("slot_list", [P, 2 * NSLOT], F32),
            "slot_index": sb("slot_index", [P, NSLOT], U32),
            "ps": [ctx.enter_context(nc.psum_tensor(f"ps{i}", [P, 512], F32)) for i in range(BANKS)],
        }
        attn = phase1(nc, ctx, a, Y, shared, at)
        phase2(nc, ctx, a, Y, shared, at, attn)


def phase1(nc, ctx, a, Y, shared, at):
    out = a["out"]
    ident, slot_list, slot_index = shared["ident"], shared["slot_list"], shared["slot_index"]
    ps = shared["ps"]

    def sb(name, shape, dt):
        return ctx.enter_context(nc.sbuf_tensor(name, shape, dt))

    def sem(name):
        return ctx.enter_context(nc.semaphore(name))

    BANK = {"Y1T": (0, 1, 2, 3), "V": (4, 5, 6, 7), "Y2T": (0, 1, 2, 3), "L": (0,), "Q": (4, 5, 6, 7),
            "G": (1,), "YT": (2, 3, 4, 5), "T": (6, 7, 0, 1), "SC": (2, 3, 4, 5), "X": (6,), "M": (7,),
            "PT": (0, 1, 2, 3), "A": (5, 6, 7, 0), "PV": (1, 2, 3, 4), "Z": (5,),
            "W": (5, 6, 7, 0), "KR": (4,), "QB": (2,)}
    LAST_BANK = {"Y2T": (5, 6, 7, 4), "L": (4,), "X": (5,), "Z": (4,)}

    def bank_of(step, b, i=0):
        return ps[(LAST_BANK if b == B - 1 and step in LAST_BANK else BANK)[step][i]]

    s_mm = {k: ctx.enter_context(nc.semaphore(f"s_mm_{k}")) for k in BANK}
    s_ev = {k: ctx.enter_context(nc.semaphore(f"s_ev_{k}")) for k in BANK}

    def filled(eng, step, b, i=0):
        eng.wait_ge(s_mm[step], len(BANK[step]) * b + i + 1)

    def drained(eng, step, b, i=0):
        if 0 <= b < B:
            eng.wait_ge(s_ev[step], len(BANK[step]) * b + i + 1)

    WH, WL = at(22, [NC, D], F32R), at(26, [NC, D], F32R)
    VWH, VWL = at(30, [NC, D], F32R), at(34, [NC, D], F32R)
    QT = at(0, [H, H, P])
    CT = at(4, [H, H * P])
    key_row, bv_all = at(50, [D]), at(51, [D])
    rw = sb("rw", [P, NC, E], F32)
    rb_all = sb("rb_all", [P, E], F32)
    bias_col = sb("bias_col", [P, 2 * NC], F32)
    qbias = sb("qbias", [P, 2 * NC + 1], F32)
    before = sb("before", [P, P], BF16)
    ones = sb("ones", [P, P], BF16)
    iota_lo = sb("iota_lo", [P, P], F32)
    iota_e = sb("iota_e", [P, E], F32)
    token_no = sb("token_no", [P, B * NT], F32)
    pad_no = sb("pad_no", [P, NSLOT], F32)
    magic = sb("magic", [P, NT], I32)
    x = [at(row, [NT, D]) for row in (46, 92, 18)]
    y = at(38, [NT, D])
    yT = at(8, [NC, S])
    G = at(12, [H * P])
    M = at(13, [H * P])
    y1h, y1l = at(68, [NC, S], F32R), at(72, [NC, S], F32R)
    qh, ql = at(52, [NC, S], F32R), at(56, [NC, S], F32R)
    wk_raw = at(52, [NC, D])
    wq_raw, wv_raw = at(88, [NC, D]), at(84, [NC, D])
    krow_products = at(56, [NT, D])
    craw = at(14, [NC, S])
    ch, cl = at(60, [NC, S], F32R), at(64, [NC, S], F32R)
    vh, vl = at(76, [NT, D], F32R), at(80, [NT, D], F32R)
    prob = at(88, [NT, S])
    ph, pl = y1h, y1l
    y2 = at(84, [NT, D])
    stats = sb("stats", [P, NT, 6], F32)
    mv = sb("mv", [P, NT, 2], F32)
    veps, rt = sb("veps", [P, NT], F32), sb("rt", [P, NT], F32)
    rstd = [sb(f"rstd{k}", [P, NT], F32) for k in range(3)]
    shift = [sb(f"shift{k}", [P, NT], F32) for k in range(3)]
    krow, smax, mr, nbias, rsum, rinv = (sb(n, [P, NT], F32) for n in ("krow", "smax", "mr", "nbias", "rsum", "rinv"))
    lg = sb("lg", [P, NT, E], F32)
    lmax, lsum, linv = (sb(n, [P, NT], F32) for n in ("lmax", "lsum", "linv"))
    top = sb("top", [P, NT, 8], F32)
    topi = sb("topi", [P, NT, 8], U32)
    eidx = sb("eidx", [P, NT, K], F32)
    oh = sb("oh", [P, K, NT, E], F32)
    picked = sb("picked", [P, NT, E], BF16)
    count = sb("count", [P, E], BF16)
    pos2 = sb("pos2", [P, K, NT, E], F32)
    pos = sb("pos", [P, K, NT], F32)
    slot = sb("slot", [P, K, NT], F32)
    slot_i = sb("slot_i", [P, K, NT], I32)
    hi_i, lo_i = sb("hi_i", [P, K, NT], I32), sb("lo_i", [P, K, NT], I32)
    slot_hi, slot_lo = sb("slot_hi", [P, K, NT], F32), sb("slot_lo", [P, K, NT], F32)
    idw = sb("idw", [P, K, NT], F32)
    gate = sb("gate", [P, K, NT], F32)
    oh_lo = [at(42 + i / 4, [P]) for i in range(K * NT)]
    oh_hi = [sb(f"oh_hi{i}", [P, 2 * NSLOT], F32) for i in range(K * NT)]

    s_w, s_small = sem("s_w"), sem("s_small")
    s_wqk, s_wv = [sem(f"s_wqk{j}") for j in range(NC)], sem("s_wv")
    s_x = [sem(f"s_x{i}") for i in range(XS)]
    s_c = sem("s_c")
    s_const, s_pool = sem("s_const"), sem("s_pool")
    s_bkb, s_init, s_wh, s_whi = sem("s_bkb"), sem("s_init"), sem("s_wh"), sem("s_whi")
    s_y0, s_y1, s_y1h = sem("s_y0"), sem("s_y1"), sem("s_y1h")
    s_ch, s_cl = sem("s_ch"), sem("s_cl")
    s_vh = sem("s_vh")
    s_qh, s_nb, s_ph = sem("s_qh"), sem("s_nb"), sem("s_ph")
    s_y2, s_base, s_xb = sem("s_y2"), sem("s_base"), sem("s_xb")
    s_stat = [sem(f"s_stat{k}") for k in range(3)]
    s_krow, s_index = sem("s_krow"), sem("s_index")
    s_lg, s_le, s_pick = sem("s_lg"), sem("s_le"), sem("s_pick")
    s_oh = sem("s_oh")
    s_out, s_yout = sem("s_out"), sem("s_yout")
    s_zero, s_pad = sem("s_zero"), sem("s_pad")
    s_dve = sem("s_dve")
    s_count, s_cnt = sem("s_count"), sem("s_cnt")

    def sync(sp):
        def load_x(b):
            if b >= XS:
                sp.wait_ge(s_out, 16 * (b - XS + 1))
            sp.dma_start(x[b % XS][:], a["x"][b].rearrange("(t p) d -> p t d", p=P)).then_inc(s_x[b % XS], 16)

        for dst, src in ((bias_col[:, 0:NC], a["bq"].rearrange("(c p) -> p c", p=P)),
                         (bias_col[:, NC:2 * NC], a["bk"].rearrange("(c p) -> p c", p=P)),
                         (bv_all[:], a["bv"].partition_broadcast(P)),
                         (rb_all[:], a["rb"].partition_broadcast(P)),
                         (rw[:], a["rw"].rearrange("(c p) e -> p c e", p=P))):
            with nc.allow_non_contiguous_dma(reason="a few columns of biases"):
                sp.dma_start(dst, src).then_inc(s_small, 16)
        for j in range(NC):
            rows = slice(j * P, (j + 1) * P)
            sp.dma_start(wq_raw[:, j, :], a["WqT"][rows, :]).then_inc(s_wqk[j], 16)
            sp.dma_start(wk_raw[:, j, :], a["WkT"][rows, :]).then_inc(s_wqk[j], 16)
            if j == NC - 2:
                load_x(0)
        sp.dma_start(wv_raw[:], a["Wv"].rearrange("(c p) n -> p c n", p=P)).then_inc(s_wv, 16)
        sp.dma_start(CT[:], a["CT"]).then_inc(s_w, 16)
        sp.dma_start(QT[:], a["QT"]).then_inc(s_w, 16)

        def step(name, b):
            if name == "C":
                if b >= 1:
                    sp.wait_ge(s_cl, NC * b)
                sp.dma_start(craw[:], a["ctxT"][b].rearrange("(c p) k -> p c k", p=P)).then_inc(s_c, 16)
                if b == 0:
                    for first in range(1, XS):
                        load_x(first)
            if name == "PV":
                rows = slice(b * S, (b + 1) * S)
                sp.wait_ge(s_y2, NT * (b + 1))
                sp.wait_ge(s_yout, 16 * b)
                sp.dma_start(Y[rows, :].rearrange("(t p) d -> p t d", p=P), y2[:]).then_inc(s_yout, 16)
                sp.wait_ge(s_base, NT * (b + 1))
                sp.wait_ge(s_out, 16 * b)
                sp.dma_start(out[rows, :].rearrange("(t p) d -> p t d", p=P), x[b % XS][:]).then_inc(s_out, 16)
                if b + XS < B:
                    load_x(b + XS)
        return step

    def gpsimd(pool):
        n_pool = [0]

        def link(ins):
            n_pool[0] += 1
            ins.then_inc(s_pool, 1)
            pool.wait_ge(s_pool, n_pool[0])

        link(pool.memset(ident[:], 0.0))
        pool.affine_select(out=ident[:], in_=ident[:], compare_op=ALU.not_equal, fill=1.0, base=0,
                           pattern=[[-1, P]], channel_multiplier=1).then_inc(s_const, 1)
        link(pool.memset(before[:], 1.0))
        pool.affine_select(out=before[:], in_=before[:], compare_op=ALU.is_gt, fill=0.0, base=0,
                           pattern=[[1, P]], channel_multiplier=-1).then_inc(s_const, 1)
        pool.memset(ones[:], 1.0).then_inc(s_const, 1)
        pool.memset(count[:], 0.0).then_inc(s_const, 1)
        pool.memset(slot_list[:], 0.0).then_inc(s_const, 1)
        pool.memset(magic[:], 0x5F3759E0).then_inc(s_const, 1)
        pool.iota(iota_lo[:], [[1, P]], 0, 0, True).then_inc(s_const, 1)
        pool.iota(iota_e[:], [[1, E]], 0, 0, True).then_inc(s_const, 1)
        pool.iota(token_no[:], [[P, B * NT]], 0, 1, True).then_inc(s_const, 1)
        pool.iota(pad_no[:], [[0, E], [P, ET]], N, 1, True).then_inc(s_const, 1)
        pool.memset(vh[:, 0, :].bitcast(F32), 0.0).then_inc(s_zero, 1)
        pool.wait_ge(s_zero, 1)
        for dst in (Y, out):
            pool.dma_start(dst[N:N + PAD, :].rearrange("(t p) d -> p t d", p=P),
                           vh[:, 0, :].bitcast(F32).unsqueeze(1).to_broadcast([P, PAD // P, D])).then_inc(s_pad, 16)
        pool.wait_ge(s_pad, 32)

        def step(name, b):
            if name == "C":
                if b >= 1:
                    filled(pool, "SC", b - 1, NT - 1)
                for c in range(NC):
                    pool.wait_ge(s_ch, NC * b + c + 1)
                    pool.tensor_tensor(cl[:, c, :], craw[:, c, :], ch[:, c, :].bitcast(F32),
                                       ALU.subtract).then_inc(s_cl, 1)
            if name == "PV":
                for t in range(NT):
                    pool.wait_ge(s_y2, NT * b + t + 1)
                    pool.tensor_tensor(x[b % XS][:, t, :], x[b % XS][:, t, :], y2[:, t, :],
                                       ALU.add).then_inc(s_base, 1)
            if name == "LN1":
                for t in range(NT):
                    pool.wait_ge(s_y1, NT * b + t + 1)
                    pool.tensor_tensor(x[b % XS][:, t, :], x[b % XS][:, t, :], bv_all[:], ALU.add)\
                        .then_inc(s_xb, 1)

        return step

    def scalar(act):
        def copy(dst, src):
            return act.activation(dst, src, ACT.Copy)

        def normalise(k, dst, b, done):
            act.wait_ge(s_stat[k], b + 1)
            for t in range(NT):
                act.activation(dst[:, t, :], x[b % XS][:, t, :], ACT.Identity, bias=shift[k][:, t:t + 1],
                               scale=rstd[k][:, t:t + 1]).then_inc(done, 1)

        def normalise_x2(b):
            if b >= 1:
                act.wait_ge(s_yout, 16 * b)
                act.wait_ge(s_base, NT * b)
                filled(act, "Y2T", b - 1, NC - 1)
            normalise(2, y2, b, s_y2)

        def step(name, b):
            if name == "LN0":
                if b >= 1:
                    filled(act, "Y1T", b - 1, NC - 1)
                    act.wait_ge(s_krow, b)
                normalise(0, y, b, s_y0)
            if name == "T":
                for q in range(H):
                    filled(act, "T", b, q)
                    bank = bank_of("T", b, q)
                    copy(y[:, q, :], bank[:]).then_inc(s_ev["T"], 1)
            if name == "M":
                filled(act, "M", b)
                bank = bank_of("M", b, 0)
                copy(M[:], bank[:]).then_inc(s_ev["M"], 1)
            if name == "LN1":
                filled(act, "M", b)
                normalise(1, y, b, s_y1)
            if name == "LN2" and b == B - 1:
                normalise_x2(b)
            if name == "WV":
                act.wait_ge(s_wv, 16)
                for c in range(NC):
                    copy(VWH[:, c, :], wv_raw[:, c, :]).then_inc(s_wh, 1)
            if name == "INIT":
                for c in range(NC):
                    filled(act, "W", 0, c)
                    bank = bank_of("W", b, c)
                    copy(WH[:, c, :], bank[:]).then_inc(s_whi, 1)
            if name == "Y1T":
                for c in range(NC):
                    filled(act, "Y1T", b, c)
                    bank = bank_of("Y1T", b, c)
                    copy(y1h[:, c, :], bank[:]).then_inc(s_y1h, 1)
            if name == "Y2T":
                for c in range(NC):
                    filled(act, "Y2T", b, c)
                    bank = bank_of("Y2T", b, c)
                    copy(prob[:, c, :], bank[:]).then_inc(s_ev["Y2T"], 1)
            if name == "L":
                act.wait_ge(s_lg, b + 1)
                for t in range(NT):
                    act.activation(lg[:, t, :], lg[:, t, :], ACT.Exp, bias=lmax[:, t:t + 1],
                                   accum_out=lsum[:, t:t + 1]).then_inc(s_le, 1)
            if name == "Q":
                for c in range(NC):
                    filled(act, "Q", b, c)
                    bank = bank_of("Q", b, c)
                    act.activation(qh[:, c, :], bank[:], ACT.Identity, bias=qbias[:, 2 * c:2 * c + 1])\
                       .then_inc(s_qh, 1)
            if name == "G":
                filled(act, "G", b)
                bank = bank_of("G", b, 0)
                copy(G[:], bank[:]).then_inc(s_ev["G"], 1)
                for c in range(NC):
                    filled(act, "YT", b, c)
                    bank = bank_of("YT", b, c)
                    copy(yT[:, c, :], bank[:]).then_inc(s_ev["YT"], 1)
            if name == "SC":
                for t in range(NT):
                    act.wait_ge(s_nb, NT * b + t + 1)
                    filled(act, "SC", b, t)
                    bank = bank_of("SC", b, t)
                    act.activation(prob[:, t, :], bank[:], ACT.Exp, bias=nbias[:, t:t + 1],
                                         scale=SCALE, accum_out=rsum[:, t:t + 1]).then_inc(s_ev["SC"], 1)
            if name == "PT":
                for c in range(NT):
                    filled(act, "PT", b, c)
                    bank = bank_of("PT", b, c)
                    copy(ph[:, c, :], bank[:]).then_inc(s_ph, 1)
            if name == "C":
                act.wait_ge(s_c, 16 * (b + 1))
                if b >= 1:
                    filled(act, "SC", b - 1, NT - 1)
                for c in range(NC):
                    copy(ch[:, c, :], craw[:, c, :]).then_inc(s_ch, 1)
            if name == "V":
                for t in range(NT):
                    filled(act, "V", b, t)
                    bank = bank_of("V", b, t)
                    copy(vh[:, t, :], bank[:]).then_inc(s_vh, 1)
                    if t == 1 and b >= 1:
                        normalise_x2(b - 1)

        return step

    def vector(dve):
        n_dve = [0]

        def link(ins):
            n_dve[0] += 1
            ins.then_inc(s_dve, 1)
            dve.wait_ge(s_dve, n_dve[0])

        def inverse_deviation(k):
            link(dve.tensor_scalar(veps[:], mv[:, :, 1], EPS, None, ALU.add))
            link(dve.tensor_scalar(rstd[k][:].bitcast(I32), veps[:].bitcast(I32), 1, -1,
                                   ALU.logical_shift_right, ALU.bitwise_xor))
            link(dve.tensor_tensor(rstd[k][:].bitcast(I32), rstd[k][:].bitcast(I32), magic[:], ALU.add))
            for _ in range(3):
                link(dve.tensor_tensor(rt[:], rstd[k][:], rstd[k][:], ALU.mult))
                link(dve.scalar_tensor_tensor(rt[:], rt[:], -0.5, veps[:], ALU.mult, ALU.mult))
                link(dve.scalar_tensor_tensor(rstd[k][:], rt[:], 1.5, rstd[k][:], ALU.add, ALU.mult))

        def deviations(k, b, used):
            src = x[b % XS]
            for t in range(NT):
                last = dve.bn_stats(stats[:, t, :], src[:, t, :])
            link(last)
            for t in range(NT):
                last = dve.bn_aggr(mv[:, t, :], stats[:, t, :])
            link(last)
            dve.wait_ge(used, NT * b)
            inverse_deviation(k)
            dve.scalar_tensor_tensor(shift[k][:], mv[:, :, 0], -1.0, rstd[k][:], ALU.mult, ALU.mult)\
                .then_inc(s_stat[k], 1)

        dve.wait_ge(s_const, 10)
        dve.wait_ge(s_small, 16 * 5)
        for c in range(NC):
            last = dve.tensor_copy(M[:, c * P:(c + 1) * P], bias_col[:, NC + c:NC + c + 1].to_broadcast([P, P]))
        last.then_inc(s_bkb, 1)

        def step(name, b):
            if name == "INIT":
                for c in range(NC):
                    dve.wait_ge(s_whi, c + 1)
                    filled(dve, "W", 0, c)
                    bank = bank_of("W", b, c)
                    dve.tensor_tensor(WL[:, c, :], bank[:], WH[:, c, :].bitcast(F32), ALU.subtract)\
                        .then_inc(s_ev["W"], 1)
                filled(dve, "KR", 0)
                bank = bank_of("KR", b, 0)
                dve.tensor_copy(key_row[:], bank[:]).then_inc(s_ev["KR"], 1)
            if name == "WV":
                for c in range(NC):
                    dve.wait_ge(s_wh, c + 1)
                    last = dve.tensor_tensor(VWL[:, c, :], wv_raw[:, c, :], VWH[:, c, :].bitcast(F32), ALU.subtract)
                last.then_inc(s_wh, 1)
            if name == "QB":
                filled(dve, "QB", 0)
                bank = bank_of("QB", b, 0)
                dve.tensor_copy(qbias[:], bank[:, 0:2 * NC + 1]).then_inc(s_ev["QB"], 1)
                drained(dve, "QB", 0)
            if name == "LN0":
                dve.wait_ge(s_x[b % XS], 16 * (b // XS + 1))
                deviations(0, b, s_y0)
            if name == "A":
                for t in range(NT):
                    filled(dve, "A", b, t)
                    bank = bank_of("A", b, t)
                    dve.tensor_tensor(x[b % XS][:, t, :], bank[:], x[b % XS][:, t, :], ALU.add).then_inc(s_ev["A"], 1)
            if name == "LN1":
                drained(dve, "A", b, NT - 1)
                deviations(1, b, s_y1)
            if name == "V":
                for t in range(NT):
                    dve.wait_ge(s_vh, NT * b + t + 1)
                    bank = bank_of("V", b, t)
                    dve.tensor_tensor(vl[:, t, :], bank[:], vh[:, t, :].bitcast(F32), ALU.subtract)\
                        .then_inc(s_ev["V"], 1)
            if name == "KROW":
                dve.wait_ge(s_y1, NT * (b + 1))
                if b >= 1:
                    filled(dve, "PT", b - 1, NT - 1)
                for t in range(NT):
                    last = dve.tensor_tensor_reduce(krow_products[:, t, :], y[:, t, :], key_row[:], 1.0, 0.0,
                                                    ALU.mult, ALU.add, krow[:, t:t + 1])
                link(last)
                dve.tensor_scalar(krow[:], krow[:], qbias[:, 2 * NC:2 * NC + 1], None, ALU.add)\
                    .then_inc(s_krow, 1)
            if name == "Y1T":
                for c in range(NC):
                    dve.wait_ge(s_y1h, NC * b + c + 1)
                    filled(dve, "Y1T", b, c)
                    bank = bank_of("Y1T", b, c)
                    dve.tensor_tensor(y1l[:, c, :], bank[:], y1h[:, c, :].bitcast(F32), ALU.subtract)\
                        .then_inc(s_ev["Y1T"], 1)
            if name == "Q":
                for c in range(NC):
                    dve.wait_ge(s_qh, NC * b + c + 1)
                    filled(dve, "Q", b, c)
                    bank = bank_of("Q", b, c)
                    dve.scalar_tensor_tensor(ql[:, c, :], bank[:], qbias[:, 2 * c:2 * c + 1],
                                               qh[:, c, :].bitcast(F32), ALU.add, ALU.subtract)\
                        .then_inc(s_ev["Q"], 1)
            if name == "SC":
                dve.wait_ge(s_krow, b + 1)
                for t in range(NT):
                    filled(dve, "SC", b, t)
                    bank = bank_of("SC", b, t)
                    link(dve.reduce_max(smax[:, t:t + 1], bank[:], AX_X))
                    link(dve.tensor_tensor(mr[:, t:t + 1], smax[:, t:t + 1], krow[:, t:t + 1], ALU.add))
                    dve.tensor_scalar(nbias[:, t:t + 1], mr[:, t:t + 1], krow[:, t:t + 1], -SCALE,
                                      ALU.subtract, ALU.mult).then_inc(s_nb, 1)
            if name == "PT":
                for c in range(NT):
                    dve.wait_ge(s_ph, NT * b + c + 1)
                    filled(dve, "PT", b, c)
                    bank = bank_of("PT", b, c)
                    dve.tensor_tensor(pl[:, c, :], bank[:], ph[:, c, :].bitcast(F32), ALU.subtract)\
                        .then_inc(s_ev["PT"], 1)
            if name == "PV":
                drained(dve, "SC", b, NT - 1)
                link(dve.reciprocal(rinv[:], rsum[:]))
                for t in range(NT):
                    filled(dve, "PV", b, t)
                    dve.wait_ge(s_xb, NT * b + t + 1)
                    bank = bank_of("PV", b, t)
                    dve.scalar_tensor_tensor(x[b % XS][:, t, :], bank[:], rinv[:, t:t + 1],
                                                   x[b % XS][:, t, :], ALU.mult, ALU.add).then_inc(s_ev["PV"], 1)
            if name == "LN2":
                drained(dve, "PV", b, NT - 1)
                deviations(2, b, s_y2)
            if name == "L":
                filled(dve, "L", b)
                bank = bank_of("L", b, 0)
                dve.tensor_tensor(lg[:], bank[:, 0:NT * E].rearrange("p (t e) -> p t e", e=E),
                                  rb_all[:].unsqueeze(1).to_broadcast([P, NT, E]), ALU.add)\
                    .then_inc(s_ev["L"], 1)
                drained(dve, "L", b)
                dve.tensor_reduce(lmax[:], lg[:], AX_X, ALU.max, negate=True).then_inc(s_lg, 1)
                dve.wait_ge(s_le, NT * (b + 1))
                link(dve.reciprocal(linv[:], lsum[:]))
                link(dve.tensor_tensor(lg[:], lg[:], linv[:].unsqueeze(2).to_broadcast([P, NT, E]), ALU.mult))
                for t in range(NT):
                    last = dve.max(top[:, t, :], lg[:, t, :])
                link(last)
                for t in range(NT):
                    last = dve.max_index(topi[:, t, :], top[:, t, :], lg[:, t, :])
                link(last)
                link(dve.tensor_copy(eidx[:], topi[:, :, 0:K]))
                for k in range(K):
                    last = dve.tensor_tensor(oh[:, k], iota_e[:].unsqueeze(1).to_broadcast([P, NT, E]),
                                             eidx[:, :, k:k + 1].to_broadcast([P, NT, E]), ALU.is_equal)
                link(last)
                dve.tensor_tensor(picked[:], oh[:, 0], oh[:, 1], ALU.add).then_inc(s_pick, 1)
                link(dve.tensor_tensor(linv[:], top[:, :, 0], top[:, :, 1], ALU.add))
                link(dve.tensor_scalar(linv[:], linv[:], 1e-9, None, ALU.add))
                link(dve.reciprocal(linv[:], linv[:]))
                for k in range(K):
                    dve.tensor_tensor(gate[:, k, :], top[:, :, k], linv[:], ALU.mult).then_inc(s_count, 1)
            if name == "X":
                filled(dve, "X", b)
                bank = bank_of("X", b, 0)
                for k in range(K):
                    last = dve.tensor_tensor(pos2[:, k], bank[:, 0:NT * E].rearrange("p (t e) -> p t e", e=E),
                                             oh[:, k], ALU.mult)
                last.then_inc(s_ev["X"], 1)
                drained(dve, "X", b)
                link(dve.tensor_reduce(pos[:], pos2[:], AX_X, ALU.add))
                link(dve.tensor_scalar(slot[:], pos[:], float(CAP), float(1 << 16), ALU.is_ge, ALU.mult))
                link(dve.tensor_tensor(slot[:], slot[:], pos[:], ALU.add))
                for k in range(K):
                    last = dve.scalar_tensor_tensor(slot[:, k], eidx[:, :, k], float(CAP), slot[:, k],
                                                    ALU.mult, ALU.add)
                link(last)
                link(dve.tensor_copy(slot_i[:], slot[:]))
                dve.tensor_scalar(lo_i[:], slot_i[:], P - 1, None, ALU.bitwise_and)
                link(dve.tensor_scalar(hi_i[:], slot_i[:], 7, None, ALU.logical_shift_right))
                dve.tensor_copy(slot_lo[:], lo_i[:]).then_inc(s_count, 1)
                dve.tensor_copy(slot_hi[:], hi_i[:]).then_inc(s_count, 1)
                for k in range(K):
                    last = dve.scalar_tensor_tensor(idw[:, k], pos[:, k], -1.0,
                                                    token_no[:, b * NT:(b + 1) * NT], ALU.mult, ALU.add)
                link(last)
                dve.tensor_scalar(idw[:], idw[:], -float(N), None, ALU.add).then_inc(s_count, 1)
                for t in range(NT):
                    last = dve.tensor_tensor(count[:], count[:], picked[:, t, :], ALU.add)
                    if t < NT - 1:
                        link(last)
                last.then_inc(s_cnt, 1)
                dve.wait_ge(s_cnt, b + 1)
            if name == "ONEHOT":
                if b >= 1:
                    filled(dve, "Z", b - 1)
                dve.wait_ge(s_count, 5 * (b + 1))
                for n in range(K * NT):
                    k, t = divmod(n, NT)
                    hi = slot_hi[:, k, t:t + 1]
                    dve.tensor_scalar(oh_lo[n][:], iota_lo[:], slot_lo[:, k, t:t + 1], None,
                                      ALU.is_equal).then_inc(s_oh, 1)
                    dve.tensor_scalar(oh_hi[n][:, 0:NSLOT], iota_lo[:, 0:NSLOT], hi,
                                      idw[:, k, t:t + 1], ALU.is_equal, ALU.mult).then_inc(s_oh, 1)
                    dve.tensor_scalar(oh_hi[n][:, NSLOT:2 * NSLOT], iota_lo[:, 0:NSLOT], hi,
                                      gate[:, k, t:t + 1], ALU.is_equal, ALU.mult).then_inc(s_oh, 1)
            if name == "Z":
                filled(dve, "Z", b)
                bank = bank_of("Z", b, 0)
                dve.tensor_tensor(slot_list[:], bank[:, 0:2 * NSLOT], slot_list[:], ALU.add).then_inc(s_ev["Z"], 1)
                drained(dve, "Z", b)
                if b == B - 1:
                    dve.tensor_tensor(slot_index[:], slot_list[:, 0:NSLOT], pad_no[:], ALU.add)\
                        .then_inc(s_index, 1)
        return step

    def tensor(pe):
        def f32_group(out, pairs):
            for i, (left, right) in enumerate(pairs):
                last = pe.matmul(out, left, right, start=(i == 0), stop=(i == len(pairs) - 1))
            return last

        def transposes(step, b, src, c):
            for t in range(NT):
                last = pe.transpose(bank_of(step, b, c)[:, t * P:(t + 1) * P], src[:, t, c * P:(c + 1) * P],
                                    ident[:])
            last.then_inc(s_mm[step], 1)

        def logit_products(b):
            def product(t, c):
                ins = pe.matmul(bank_of("L", b)[:, t * E:(t + 1) * E], prob[:, c, t * P:(t + 1) * P], rw[:, c, :],
                                start=(c == 0), stop=(c == NC - 1))
                if (t, c) == (NT - 1, NC - 1):
                    ins.then_inc(s_mm["L"], 1)
            return [lambda t=t, c=c: product(t, c) for t in range(NT) for c in range(NC)]

        pe.wait_ge(s_const, 10)

        def step(name, b):
            if name == "INIT":
                for j in range(NC):
                    pe.wait_ge(s_wqk[j], 32)
                    for c in range(NC):
                        last = pe.matmul(bank_of("W", b, c)[:], wq_raw[:, j, c * P:(c + 1) * P], wk_raw[:, j, :],
                                         start=(j == 0), stop=(j == NC - 1))
                        if j == NC - 1:
                            last.then_inc(s_mm["W"], 1)
                pe.wait_ge(s_bkb, 1)
                pe.wait_ge(s_small, 16 * 5)
                f32_group(bank_of("KR", b)[:], [(M[:, j * P:(j + 1) * P], wq_raw[:, j, :])
                                                for j in range(NC)]).then_inc(s_mm["KR"], 1)
            if name == "QB":
                drained(pe, "YT", 0, 0)
                bank = bank_of("QB", b)
                for c in range(NC):
                    f32_group(bank[:, 2 * c:2 * c + 2],
                              [(wk_raw[:, j, c * P:(c + 1) * P], bias_col[:, j:j + 2]) for j in range(NC)])
                f32_group(bank[:, 2 * NC:2 * NC + 1], [(M[:, j * P:(j + 1) * P], bias_col[:, j:j + 1])
                                                       for j in range(NC)]).then_inc(s_mm["QB"], 1)
            if name == "V":
                if b == 0:
                    pe.wait_ge(s_wh, NC + 1)
                pe.wait_ge(s_cl, NC * (b + 1))
                drained(pe, "PV", b - 1, 3)
                drained(pe, "A", b, 2)
                for t in range(NT):
                    if t == 1:
                        drained(pe, "Z", b - 2)
                    cols = slice(t * P, (t + 1) * P)
                    parts = [(ch[:, c, cols], cl[:, c, cols], VWH[:, c, :], VWL[:, c, :]) for c in range(NC)]
                    three_pass(pe, bank_of("V", b, t)[:], parts).then_inc(s_mm["V"], 1)
            if name == "Y1T":
                pe.wait_ge(s_y1, NT * (b + 1))
                if b == 0:
                    drained(pe, "QB", 0)
                for c in range(NC):
                    if c > 0:
                        drained(pe, "PV", b - 1, c - 1)
                    transposes("Y1T", b, y, c)
            if name == "Y2T":
                pe.wait_ge(s_y2, NT * (b + 1))
                for c in range(NC):
                    drained(pe, "Y1T", b + 1, c)
                    if b == B - 1 and c == 0:
                        drained(pe, "Z", b - 1)
                    transposes("Y2T", b, y2, c)
            if name == "Q":
                drained(pe, "Y1T", b, NC - 1)
                if b == 0:
                    drained(pe, "W", 0, NC - 1)
                logits = logit_products(b - 1) if b >= 1 else []
                for c in range(NC):
                    drained(pe, "V", b, c)
                    if c == 1 and b >= 1:
                        drained(pe, "Y2T", b - 1, NC - 1)
                    cols = slice(c * P, (c + 1) * P)
                    parts = [(WH[:, j, cols], WL[:, j, cols], y1h[:, j, :], y1l[:, j, :]) for j in range(NC)]
                    three_pass(pe, bank_of("Q", b, c)[:], parts,
                               logits if c > 0 else []).then_inc(s_mm["Q"], 1)
                while logits:
                    logits.pop(0)()
            if name == "L" and b == B - 1:
                drained(pe, "Y2T", b, NC - 1)
                for product in logit_products(b):
                    product()
            if name == "G":
                pe.wait_ge(s_y0, NT * (b + 1))
                drained(pe, "Y2T", b - 2, 3)
                for q in range(H):
                    cols = slice(q * P, (q + 1) * P)
                    last = f32_group(bank_of("G", b)[:, cols], [(y[:, t, cols], y[:, t, cols]) for t in range(NT)])
                last.then_inc(s_mm["G"], 1)
                drained(pe, "Q", b - 1, 1)
                if b == 0:
                    drained(pe, "KR", 0)
                    drained(pe, "W", 0, NC - 1)
                for c in range(NC):
                    transposes("YT", b, y, c)
            if name == "T":
                if b == 0:
                    pe.wait_ge(s_w, 32)
                drained(pe, "Q", b - 1, 3)
                drained(pe, "L", b - 2)
                drained(pe, "G", b)
                for q in range(H):
                    pe.matmul(bank_of("T", b, q)[:], G[:, q * P:(q + 1) * P], CT[:, q, :],
                              start=True, stop=True).then_inc(s_mm["T"], 1)
            if name == "SC":
                drained(pe, "Q", b, NC - 1)
                drained(pe, "YT", b + 1, 3)
                for t in range(NT):
                    cols = slice(t * P, (t + 1) * P)
                    three_pass(pe, bank_of("SC", b, t)[:], [(qh[:, c, cols], ql[:, c, cols], ch[:, c, :], cl[:, c, :])
                                                            for c in range(NC)]).then_inc(s_mm["SC"], 1)
            if name == "X":
                pe.wait_ge(s_pick, b + 1)
                drained(pe, "T", b + 2, 0)
                pe.wait_ge(s_cnt, b)
                for t in range(NT):
                    pairs = [(before[:], picked[:, t, :])] + [(ones[:], picked[:, i, :]) for i in range(t)]
                    last = f32_group(bank_of("X", b)[:, t * E:(t + 1) * E], pairs + [(ones[:], count[:])])
                last.then_inc(s_mm["X"], 1)
            if name == "M":
                drained(pe, "T", b, H - 1)
                for h in range(H):
                    cols = slice(h * P, (h + 1) * P)
                    last = f32_group(bank_of("M", b)[:, cols], [(QT[:, h, q, :], y[:, q, cols]) for q in range(H)])
                last.then_inc(s_mm["M"], 1)
            if name == "PT":
                drained(pe, "SC", b, NT - 1)
                drained(pe, "T", b + 1, 3)
                for c in range(NT):
                    transposes("PT", b, prob, c)
            if name == "A":
                drained(pe, "M", b)
                drained(pe, "YT", b, NC - 1)
                drained(pe, "SC", b - 1, 3)
                drained(pe, "X", b - 2)
                for t in range(NT):
                    if t == NT - 1:
                        drained(pe, "PT", b - 1, 0)
                    for h in range(H):
                        cols = slice(h * P, (h + 1) * P)
                        last = pe.matmul(bank_of("A", b, t)[:, cols], yT[:, h, t * P:(t + 1) * P], M[:, cols],
                                         start=True, stop=True)
                    last.then_inc(s_mm["A"], 1)
            if name == "PV":
                drained(pe, "PT", b, NT - 1)
                for t in range(NT):
                    cols = slice(t * P, (t + 1) * P)
                    three_pass(pe, bank_of("PV", b, t)[:], [(ph[:, c, cols], pl[:, c, cols], vh[:, c, :], vl[:, c, :])
                                                            for c in range(NT)]).then_inc(s_mm["PV"], 1)
            if name == "Z":
                drained(pe, "A", b + 2, 0)
                for n in range(K * NT):
                    pe.wait_ge(s_oh, 3 * (K * NT * b + n + 1))
                    last = pe.matmul(bank_of("Z", b)[:, 0:2 * NSLOT], oh_lo[n][:], oh_hi[n][:],
                                     start=(n == 0), stop=(n == K * NT - 1))
                last.then_inc(s_mm["Z"], 1)
        return step

    return {"sync": sync, "gpsimd": gpsimd, "scalar": scalar, "vector": vector, "tensor": tensor,
            "filled": filled, "drained": drained, "s_cl": s_cl, "s_krow": s_krow, "s_xb": s_xb, "s_base": s_base,
            "s_yout": s_yout, "s_out": s_out, "s_index": s_index}


def phase2(nc, ctx, a, Y, shared, at, attn):
    out = a["out"]
    ident, slot_list, slot_index = shared["ident"], shared["slot_list"], shared["slot_index"]
    filled, drained = attn["filled"], attn["drained"]
    RING = 22
    RAW = 6
    TMP = 3

    def sem(name):
        return ctx.enter_context(nc.semaphore(name))

    ps = shared["ps"]
    gate_bank = [ps[0], ps[2]]
    up_bank = [ps[1], ps[3]]
    down_bank = [ps[4], ps[5]]
    x_bank = [ps[6], ps[7]]
    wraw = [at(i, [D]) for i in range(RAW)]
    wh = [at(6 + 2 * i, [D], F32R) for i in range(RING)]
    wl = [at(7 + 2 * i, [D], F32R) for i in range(RING)]
    xn = [at(52, [ET, D]), at(84, [ET, D])]
    xh, xl = at(57, [NC, CAP], F32R), at(62, [NC, CAP], F32R)
    hh, hl = at(68, [FC, CAP], F32R), at(75.5, [FC - 1, CAP], F32R)
    silu = [at(row, [512]) for row in (50, 67, 83)]
    ht = [at(row, [512]) for row in (96, 97, 51)]
    ost = at(89, [ET, D])

    s_raw = [sem(f"t_raw{i}") for i in range(RAW)]
    s_wh, s_wl = sem("t_wh"), sem("t_wl")
    s_xn = [sem("t_xn0"), sem("t_xn1")]
    s_xg = [sem("t_xg0"), sem("t_xg1")]
    s_xT, s_xh, s_xl = sem("t_xT"), sem("t_xh"), sem("t_xl")
    s_gu, s_silu, s_ht, s_hh, s_hl = sem("t_gu"), sem("t_silu"), sem("t_ht"), sem("t_hh"), sem("t_hl")
    s_down, s_ost = sem("t_down"), sem("t_ost")
    s_add = [sem(f"t_add{i}") for i in range(ET)]

    groups = [(0, g, NT, g == B - 1) for g in range(B)] + [(1 + e, e, ET, True) for e in range(E)]
    NG = len(groups)
    tiles_of = [tiles for _, _, tiles, _ in groups]
    tiles_before = [sum(tiles_of[:g]) for g in range(NG + 1)]

    def cuts(g):
        n = tiles_of[g] * P
        return [(0, n)] if n <= 512 else [(0, n // 2), (n // 2, n // 2)]

    units = [(g, c, j) for g in range(NG) for c in range(FC) for j in range(len(cuts(g)))]
    unit_no = {u: n for n, u in enumerate(units)}
    n_chunks = (1 + E) * WC
    FIRST = RING - RAW

    ahead = {"V": [("WEIGHTS", (0, 2))], "Q": [("WEIGHTS", (2, 6)), ("WEIGHTS", (6, 8))], "SC": [("LOAD", 0)],
             "PT": [("TOKENS", 0), ("WEIGHTS", (8, FIRST))]}
    order = []
    for i in range(-1, B):
        steps = [("Y1T", i), ("V", i), ("KROW", i), ("Y2T", i - 1), ("LN0", i + 1), ("INIT", i + 1), ("Q", i),
                 ("L", i - 1), ("G", i + 1), ("T", i + 1), ("WV", i + 1), ("QB", i + 1),
                 ("SC", i), ("X", i - 1), ("M", i + 1), ("PT", i),
                 ("C", i + 1), ("A", i + 1), ("LN1", i + 1), ("ONEHOT", i - 1), ("PV", i), ("Z", i - 1),
                 ("LN2", i)]
        if i == -1:
            steps.remove(("C", 0))
            steps.insert(steps.index(("WV", 0)), ("C", 0))
            steps.append(("V", 0))
        if i == 0:
            steps.remove(("V", 0))
        for name, b in steps:
            if 0 <= b < (1 if name in ("INIT", "WV", "QB") else B):
                order.append((name, b))
            if i == B - 1:
                order += ahead.get(name, [])
            if (name, b) == ("A", B - 1):
                order.append(("RAW", 0))

    router = {(0, 2): [("Y2T", B - 1)], (0, 3): [("L", B - 1)], (1, 0): [("X", B - 1)],
              (1, 1): [("ONEHOT", B - 1)], (1, 2): [("Z", B - 1)]}

    def ring_slot_free(eng, n):
        if n < 4:
            filled(eng, "A", B - 1, NT - 1)
        elif n < 6:
            eng.wait_ge(attn["s_cl"], NC * B)
        elif n < 8:
            eng.wait_ge(attn["s_out"], 16 * (B - 2))
        elif n < 16:
            filled(eng, "Q", B - 1, NC - 1)
        elif n < 18:
            filled(eng, "Y1T", B - 1, NC - 1)
            eng.wait_ge(attn["s_krow"], B)
        elif n < 20:
            filled(eng, "Z", B - 1)
        else:
            eng.wait_ge(attn["s_out"], 16 * (B - 1))

    def split_after(g, step):
        job, _, _, last = groups[g]
        if g == 0 and step == 0:
            return list(range(FIRST, WC))
        if g == 1 and step == 3:
            return list(range(WC, RING))
        if not last:
            return []
        done = range(GU, WC) if step == "down" else range(2 * step, min(2 * step + 2, GU))
        return [job * WC + i + RING for i in done if job * WC + i + RING < n_chunks]

    def wait_last_use(eng, n):
        job, i = divmod(n, WC)
        g = B - 1 + job
        if i < GU:
            eng.wait_ge(s_gu, unit_no[(g, i // 2, len(cuts(g)) - 1)] + 1)
        else:
            eng.wait_ge(s_down, tiles_before[g + 1])

    def adds_of(g, t):
        return sum(tiles > t for tiles in tiles_of[:g])

    def rows_of(c):
        return P if c < FC - 1 else FH

    def tail(g):
        after = tiles_of[g + 1] if g + 1 < NG else 0
        for t in range(max(tiles_of[g], after)):
            if t < after:
                yield "x", g + 1, t
            if t < tiles_of[g]:
                yield "down", g, t

    def sync(sp):
        step = attn["sync"](sp)

        def load_tokens(g):
            if g >= 2:
                sp.wait_ge(s_xT, tiles_before[g - 1])
            sp.dma_start(xn[g % 2][:, 0:NT, :], Y[g * S:(g + 1) * S, :].rearrange("(t p) d -> p t d", p=P))\
              .then_inc(s_xn[g % 2], 16)

        def load_weights(n):
            if n >= RAW:
                sp.wait_ge(s_wl, n - RAW + 1)
            elif n == 0:
                filled(sp, "M", B - 1)
            job, i = divmod(n, WC)
            sp.dma_start(wraw[n % RAW][:], a["wts"][job, :, i * D:(i + 1) * D]).then_inc(s_raw[n % RAW], 16)

        for name, b in order:
            if name == "RAW":
                for n in range(RAW):
                    load_weights(n)
            elif name == "WEIGHTS":
                for n in range(*b):
                    load_weights(n + RAW)
            elif name == "LOAD":
                filled(sp, "SC", B - 1, NT - 1)
                sp.wait_ge(attn["s_yout"], 16)
                load_tokens(0)
            elif name != "TOKENS":
                step(name, b)
        sp.wait_ge(attn["s_yout"], 16 * B)
        sp.wait_ge(attn["s_base"], NT * B)
        filled(sp, "L", B - 1)
        for g in range(1, B):
            load_tokens(g)
        for n in range(RING, n_chunks):
            load_weights(n)
        sp.wait_ge(attn["s_out"], 16 * B)

    def gpsimd(pool):
        step = attn["gpsimd"](pool)

        def split(n):
            pool.wait_ge(s_wh, n + 1)
            pool.tensor_tensor(wl[n % RING][:], wraw[n % RAW][:], wh[n % RING][:].bitcast(F32),
                               ALU.subtract).then_inc(s_wl, 1)

        def slots(e, t):
            return bass.IndirectOffsetOnAxis(ap=slot_index[:, e * ET + t:e * ET + t + 1], axis=0)

        def gather(g):
            pool.wait_ge(s_xT, tiles_before[g - 1])
            for t in range(ET):
                pool.indirect_dma_start(xn[g % 2][:, t, :], None, Y[:, :], slots(groups[g][1], t),
                                        bounds_check=N + PAD - 1).then_inc(s_xg[g % 2], 16)

        for name, b in order:
            if name == "WEIGHTS":
                for n in range(*b):
                    split(n)
            elif name not in ("RAW", "LOAD", "TOKENS"):
                step(name, b)
        for g, (job, part, tiles, last) in enumerate(groups):
            if g + 1 < NG and groups[g + 1][0] > 0:
                if g + 1 == B:
                    pool.wait_ge(attn["s_yout"], 16 * B)
                    pool.wait_ge(attn["s_index"], 1)
                gather(g + 1)
            for c in range(FC):
                for n in split_after(g, c):
                    split(n)
            for t in range(tiles):
                pool.wait_ge(s_ost, tiles_before[g] + t + 1)
                if job == 0:
                    pool.wait_ge(attn["s_out"], 16 * (part + 1))
                    pool.dma_start(out[part * S + t * P:part * S + (t + 1) * P, :], ost[:, t, :],
                                   accum_op=ALU.add).then_inc(s_add[t], 16)
                    continue
                if t == 0:
                    for i in range(ET):
                        pool.wait_ge(s_add[i], 16 * adds_of(g, i))
                pool.indirect_dma_start(out[:, :], slots(part, t), ost[:, t, :], None,
                                        bounds_check=N + PAD - 1, compute_op=ALU.add).then_inc(s_add[t], 16)
            for n in split_after(g, "down"):
                split(n)
        for i in range(ET):
            pool.wait_ge(s_add[i], 16 * adds_of(NG, i))

    def scalar(act):
        step = attn["scalar"](act)

        def copy(dst, src):
            return act.activation(dst, src, ACT.Copy)

        def split(n):
            act.wait_ge(s_raw[n % RAW], 16 * (n // RAW + 1))
            if n >= RING:
                wait_last_use(act, n - RING)
            else:
                ring_slot_free(act, n)
            copy(wh[n % RING][:], wraw[n % RAW][:]).then_inc(s_wh, 1)

        def x_hi(g, t):
            n = tiles_before[g] + t
            act.wait_ge(s_xT, n + 1)
            copy(xh[:, :, t * P:(t + 1) * P], x_bank[n % 2][:].rearrange("p (c n) -> p c n", c=NC))\
                .then_inc(s_xh, 1)

        def h_hi(u):
            g, c, j = units[u]
            first, n = cuts(g)[j]
            act.wait_ge(s_ht, u + 1)
            copy(hh[0:rows_of(c), c, first:first + n], ht[u % TMP][0:rows_of(c), 0:n]).then_inc(s_hh, 1)

        for name, b in order:
            if name == "WEIGHTS":
                for n in range(*b):
                    split(n)
            elif name == "TOKENS":
                for t in range(NT):
                    x_hi(0, t)
            elif name not in ("RAW", "LOAD"):
                step(name, b)
        act.wait_ge(attn["s_xb"], NT * B)
        for g in range(NG):
            for c in range(FC):
                for j, (first, n) in enumerate(cuts(g)):
                    u = unit_no[(g, c, j)]
                    if u >= TMP:
                        act.wait_ge(s_ht, u - TMP + 1)
                    act.wait_ge(s_gu, u + 1)
                    bank = gate_bank[u % 2] if c < FC - 1 else up_bank[u % 2]
                    act.activation(silu[u % TMP][0:rows_of(c), 0:n], bank[0:rows_of(c), 0:n], ACT.Silu)\
                       .then_inc(s_silu, 1)
                    if u > unit_no[(g, 0, 0)]:
                        h_hi(u - 1)
                    for name, b in router.get((g, c), []):
                        step(name, b)
                if c > 0:
                    for m in split_after(g, c - 1):
                        split(m)
            h_hi(u)
            for m in split_after(g, FC - 1):
                split(m)
            for what, gx, t in tail(g):
                if what == "x":
                    x_hi(gx, t)
            for m in split_after(g, "down"):
                split(m)

    def vector(dve):
        step = attn["vector"](dve)

        def x_lo(g, t):
            n = tiles_before[g] + t
            dve.wait_ge(s_xh, n + 1)
            cols = slice(t * P, (t + 1) * P)
            dve.tensor_tensor(xl[:, :, cols], x_bank[n % 2][:].rearrange("p (c n) -> p c n", c=NC),
                              xh[:, :, cols].bitcast(F32), ALU.subtract).then_inc(s_xl, 1)

        def h_lo(u):
            g, c, j = units[u]
            first, n = cuts(g)[j]
            rows = rows_of(c)
            lo = hl[:, c] if c < FC - 1 else hh[FH:P, c]
            dve.wait_ge(s_hh, u + 1)
            dve.tensor_tensor(lo[:, first:first + n], ht[u % TMP][0:rows, 0:n],
                              hh[0:rows, c, first:first + n].bitcast(F32), ALU.subtract).then_inc(s_hl, 1)

        for name, b in order:
            if name == "TOKENS":
                for t in range(NT):
                    x_lo(0, t)
            elif name not in ("RAW", "LOAD", "WEIGHTS"):
                step(name, b)
        for g, (job, part, _, _) in enumerate(groups):
            for c in range(FC):
                for j, (first, n) in enumerate(cuts(g)):
                    u = unit_no[(g, c, j)]
                    if u >= TMP:
                        dve.wait_ge(s_hl, u - TMP + 1)
                    dve.wait_ge(s_silu, u + 1)
                    rows = slice(0, P) if c < FC - 1 else slice(FH, 2 * FH)
                    dve.tensor_tensor(ht[u % TMP][0:rows_of(c), 0:n], up_bank[u % 2][rows, 0:n],
                                      silu[u % TMP][0:rows_of(c), 0:n], ALU.mult).then_inc(s_ht, 1)
                    if u > unit_no[(g, 0, 0)]:
                        h_lo(u - 1)
                    for name, b in router.get((g, c), []):
                        step(name, b)
            h_lo(u)
            for what, gx, t in tail(g):
                if what == "x":
                    x_lo(gx, t)
                    continue
                n = tiles_before[g] + t
                dve.wait_ge(s_down, n + 1)
                if n == 0:
                    dve.wait_ge(attn["s_out"], 16 * B)
                if adds_of(g, t):
                    dve.wait_ge(s_add[t], 16 * adds_of(g, t))
                if job == 0:
                    dve.tensor_copy(ost[:, t, :], down_bank[n % 2][:]).then_inc(s_ost, 1)
                else:
                    gate = NSLOT + part * ET + t
                    dve.tensor_scalar(ost[:, t, :], down_bank[n % 2][:], slot_list[:, gate:gate + 1], None,
                                      ALU.mult).then_inc(s_ost, 1)

    def tensor(pe):
        step = attn["tensor"](pe)

        def transpose_tile(g, t):
            n = tiles_before[g] + t
            if t == 0 and groups[g][0] == 0:
                pe.wait_ge(s_xn[g % 2], 16 * (g // 2 + 1))
            if groups[g][0] > 0:
                pe.wait_ge(s_xg[g % 2], 16 * ET * ((g - B) // 2 + 1))
            if n >= 2:
                pe.wait_ge(s_xl, n - 1)
            elif n == 0:
                drained(pe, "X", B - 2)
            for c in range(NC):
                ins = pe.transpose(x_bank[n % 2][:, c * P:(c + 1) * P], xn[g % 2][:, t, c * P:(c + 1) * P],
                                   ident[:])
            ins.then_inc(s_xT, 1)

        for name, b in order:
            if name == "TOKENS":
                for t in range(NT):
                    transpose_tile(0, t)
            elif name not in ("RAW", "LOAD", "WEIGHTS"):
                step(name, b)
        for g, (job, _, tiles, _) in enumerate(groups):
            base = job * WC
            pe.wait_ge(s_xl, tiles_before[g + 1])
            for c in range(FC):
                for j, (first, n) in enumerate(cuts(g)):
                    u = unit_no[(g, c, j)]
                    if u >= 2:
                        pe.wait_ge(s_ht, u - 1)
                    else:
                        drained(pe, "PV", B - 1, 2 * u)
                    cols = slice(first, first + n)
                    chunks = ([(gate_bank, 2 * c)] if c < FC - 1 else []) + [(up_bank, min(2 * c + 1, GU - 1))]
                    for bank, i in chunks:
                        m = base + i
                        pe.wait_ge(s_wl, m + 1)
                        ins = three_pass(pe, bank[u % 2][:, 0:n], [
                            (wh[m % RING][:, d * P:(d + 1) * P], wl[m % RING][:, d * P:(d + 1) * P],
                             xh[:, d, cols], xl[:, d, cols]) for d in range(NC)])
                    ins.then_inc(s_gu, 1)
                    if (g, c) == (1, 0):
                        pe.wait_ge(s_ost, NT)
                    for name, b in router.get((g, c), []):
                        step(name, b)
            for what, gx, t in tail(g):
                if what == "x":
                    transpose_tile(gx, t)
                    continue
                n = tiles_before[g] + t
                if n >= 2:
                    pe.wait_ge(s_ost, n - 1)
                if n == 0:
                    drained(pe, "L", B - 1)
                if n == NT:
                    drained(pe, "Z", B - 1)
                if n == NT + 1:
                    drained(pe, "X", B - 1)
                cols = slice(t * P, (t + 1) * P)
                for c in range(FC):
                    m = base + GU + c
                    if t == 0:
                        pe.wait_ge(s_wl, m + 1)
                        pe.wait_ge(s_hl, unit_no[(g, c, len(cuts(g)) - 1)] + 1)
                    wh_c, wl_c = wh[m % RING], wl[m % RING]
                    if c < FC - 1:
                        passes = [(hh[:, c, cols], wh_c[:]), (hh[:, c, cols], wl_c[:]), (hl[:, c, cols], wh_c[:])]
                    else:
                        passes = [(hh[:, c, cols], wh_c[:]), (hh[0:FH, c, cols], wl_c[0:FH])]
                    for i, (left, right) in enumerate(passes):
                        ins = pe.matmul(down_bank[n % 2][:], left, right, start=(c == 0 and i == 0),
                                        stop=(c == FC - 1 and i == len(passes) - 1))
                ins.then_inc(s_down, 1)

    block = ctx.enter_context(nc.Block())
    block.sync(sync)
    block.gpsimd(gpsimd)
    block.scalar(scalar)
    block.vector(vector)
    block.tensor(tensor)


def kernel(x, ctx_1024, L0_attn_queries, L0_attn_combiners, L0_xattn_Wq, L0_xattn_bq, L0_xattn_Wk, L0_xattn_bk,
           L0_xattn_Wv, L0_xattn_bv, L0_ffn_router_w, L0_ffn_router_b, L0_ffn_w_gate, L0_ffn_w_up, L0_ffn_w_down,
           L0_ffn_sw_gate, L0_ffn_sw_up, L0_ffn_sw_down):
    import numpy as np
    import concourse.bacc as bacc
    from concourse.bass_utils import run_bass_kernel_spmd

    def chunks(gate, up, down):
        j = gate.shape[0]
        full = (FC - 1) * P
        g = gate.reshape(j, NC, P, F)
        u = up.reshape(j, NC, P, F)
        pairs = np.stack([g[..., :full].reshape(j, NC, P, FC - 1, P), u[..., :full].reshape(j, NC, P, FC - 1, P)], 4)
        pairs = pairs.transpose(0, 2, 3, 4, 1, 5).reshape(j, P, (GU - 1) * D)
        mixed = np.concatenate([g[..., full:], u[..., full:]], 3).transpose(0, 2, 1, 3).reshape(j, P, D)
        d = np.concatenate([down, down[:, F - FH:]], 1).reshape(j, FC, P, D).transpose(0, 2, 1, 3)
        return np.concatenate([pairs, mixed, d.reshape(j, P, FC * D)], 2)

    q = np.asarray(L0_attn_queries).reshape(H, P, H, P)
    c = np.asarray(L0_attn_combiners).reshape(H, H, P, P)
    gate, up, down, sgate, sup, sdown = (np.asarray(w) for w in (
        L0_ffn_w_gate, L0_ffn_w_up, L0_ffn_w_down, L0_ffn_sw_gate, L0_ffn_sw_up, L0_ffn_sw_down))
    arrays = {
        "x": np.asarray(x),
        "ctxT": np.ascontiguousarray(np.asarray(ctx_1024).transpose(0, 2, 1)),
        "QT": np.ascontiguousarray(q.transpose(3, 0, 2, 1)),
        "CT": np.ascontiguousarray(c.transpose(2, 1, 0, 3)).reshape(P, H, H * P),
        "WqT": np.ascontiguousarray(np.asarray(L0_xattn_Wq).T),
        "WkT": np.ascontiguousarray(np.asarray(L0_xattn_Wk).T),
        "Wv": np.asarray(L0_xattn_Wv),
        "bq": np.asarray(L0_xattn_bq), "bk": np.asarray(L0_xattn_bk), "bv": np.asarray(L0_xattn_bv),
        "rw": np.asarray(L0_ffn_router_w), "rb": np.asarray(L0_ffn_router_b),
        "wts": np.concatenate([chunks(sgate[None], sup[None], sdown[None]), chunks(gate, up, down)], 0),
    }
    nc = bacc.Bacc("TRN2", target_bir_lowering=False, num_devices=1)
    args = {k: nc.dram_tensor(f"in_{k}", v.shape, F32, kind="ExternalInput").ap() for k, v in arrays.items()}
    args["out"] = nc.dram_tensor("out_tokens", (N + PAD, D), F32, kind="ExternalOutput").ap()
    build(nc, args)
    r = run_bass_kernel_spmd(nc, [{f"in_{k}": v for k, v in arrays.items()}], core_ids=[0])
    return r.results[0]["out_tokens"][:N].reshape(B, S, D)
```
